# Optimizing a Trainium2 kernel written in Bass

```python
import numpy as np
import jax
import jax.numpy as jnp

def _softmax(x, axis=-1):
    return jax.nn.softmax(x, axis=axis)
def _gelu(x):
    return jax.nn.gelu(x, approximate=True)
def _silu(x):
    return jax.nn.silu(x)
def _sigmoid(x):
    return jax.nn.sigmoid(x)
def _layernorm(x, axis=-1, eps=1e-5):
    m = jnp.mean(x, axis=axis, keepdims=True)
    v = jnp.var(x, axis=axis, keepdims=True)
    return (x - m) / jnp.sqrt(v + eps)
def _scatter_add(tgt, idx, src, axis=0):
    return tgt.at[idx].add(src)
def _segment_sum(src, seg, n):
    return jax.ops.segment_sum(src, seg, n)

kernel_name = 'mk_conv_seq_d1_conv_nchw64_aabca4'

def setup_inputs(seed: int = 0):
    np.random.seed(seed)
    _w = jnp.asarray
    def _rec_inputs():
        import jax
        import jax.numpy as jnp
        _gk = jax.random.key(seed)
        x = -0.0009438 + 1 * jax.random.normal(jax.random.fold_in(_gk, 1), (2, 64, 96, 96), jnp.float32)
        return x
    x = _rec_inputs()
    def _L0_conv_setup():
        import jax, jax.numpy as jnp
        import numpy as np
        from jax import lax
        EPS = 1e-05

        def group_norm1(x, g, b):
            mu = jnp.mean(x, axis=(1, 2, 3), keepdims=True)
            var = jnp.var(x, axis=(1, 2, 3), keepdims=True)
            xn = (x - mu) * lax.rsqrt(var + EPS)
            return xn * g[None, :, None, None] + b[None, :, None, None]

        def dwconv(x, w, b):
            C = x.shape[1]
            k = w.shape[-1]
            p = k // 2
            out = lax.conv_general_dilated(x, w, (1, 1), [(p, p), (p, p)], dimension_numbers=('NCHW', 'OIHW', 'NCHW'), feature_group_count=C)
            return out + b[None, :, None, None]

        def conv1x1(x, w, b):
            return jnp.einsum('oc,bchw->bohw', w, x) + b[None, :, None, None]
        key = jax.random.key(seed)
        ks = jax.random.split(key, 10)
        B, C, H, W = (2, 64, 96, 96)
        s = 0.05
        return {'x': jax.random.normal(ks[0], (B, C, H, W), jnp.float32), 'n1_g': jnp.ones((C,), jnp.float32), 'n1_b': jnp.zeros((C,), jnp.float32), 'w3': jax.random.normal(ks[1], (C, 1, 3, 3), jnp.float32) * s, 'b3': jnp.zeros((C,), jnp.float32), 'w5': jax.random.normal(ks[2], (C, 1, 5, 5), jnp.float32) * s, 'b5': jnp.zeros((C,), jnp.float32), 'w7': jax.random.normal(ks[3], (C, 1, 7, 7), jnp.float32) * s, 'b7': jnp.zeros((C,), jnp.float32), 'gate_w': jax.random.normal(ks[4], (C, C), jnp.float32) * s, 'gate_b': jnp.zeros((C,), jnp.float32), 'proj_w': jax.random.normal(ks[5], (C, C), jnp.float32) * s, 'proj_b': jnp.zeros((C,), jnp.float32), 'n2_g': jnp.ones((C,), jnp.float32), 'n2_b': jnp.zeros((C,), jnp.float32), 'q_w': jax.random.normal(ks[6], (C, C), jnp.float32) * s, 'q_b': jnp.zeros((C,), jnp.float32), 'k_w': jax.random.normal(ks[7], (C, C), jnp.float32) * s, 'k_b': jnp.zeros((C,), jnp.float32), 'v_w': jax.random.normal(ks[8], (C, C), jnp.float32) * s, 'v_b': jnp.zeros((C,), jnp.float32)}
    _L0_conv_all = _L0_conv_setup()
    _L0_conv_in = {k: v for k, v in _L0_conv_all.items() if k in ('n1_g', 'n1_b', 'w3', 'b3', 'w5', 'b5', 'w7', 'b7', 'gate_w', 'gate_b', 'proj_w', 'proj_b', 'n2_g', 'n2_b', 'q_w', 'q_b', 'k_w', 'k_b', 'v_w', 'v_b', )}
    del _L0_conv_all

    return {
        "x": x,
        "L0_conv_n1_g": _L0_conv_in["n1_g"],
        "L0_conv_n1_b": _L0_conv_in["n1_b"],
        "L0_conv_w3": _L0_conv_in["w3"],
        "L0_conv_b3": _L0_conv_in["b3"],
        "L0_conv_w5": _L0_conv_in["w5"],
        "L0_conv_b5": _L0_conv_in["b5"],
        "L0_conv_w7": _L0_conv_in["w7"],
        "L0_conv_b7": _L0_conv_in["b7"],
        "L0_conv_gate_w": _L0_conv_in["gate_w"],
        "L0_conv_gate_b": _L0_conv_in["gate_b"],
        "L0_conv_proj_w": _L0_conv_in["proj_w"],
        "L0_conv_proj_b": _L0_conv_in["proj_b"],
        "L0_conv_n2_g": _L0_conv_in["n2_g"],
        "L0_conv_n2_b": _L0_conv_in["n2_b"],
        "L0_conv_q_w": _L0_conv_in["q_w"],
        "L0_conv_q_b": _L0_conv_in["q_b"],
        "L0_conv_k_w": _L0_conv_in["k_w"],
        "L0_conv_k_b": _L0_conv_in["k_b"],
        "L0_conv_v_w": _L0_conv_in["v_w"],
        "L0_conv_v_b": _L0_conv_in["v_b"],
    }

def reference(x, L0_conv_n1_g, L0_conv_n1_b, L0_conv_w3, L0_conv_b3, L0_conv_w5, L0_conv_b5, L0_conv_w7, L0_conv_b7, L0_conv_gate_w, L0_conv_gate_b, L0_conv_proj_w, L0_conv_proj_b, L0_conv_n2_g, L0_conv_n2_b, L0_conv_q_w, L0_conv_q_b, L0_conv_k_w, L0_conv_k_b, L0_conv_v_w, L0_conv_v_b):
    import jax
    import jax.numpy as jnp
    def _L0_conv_ref(x, n1_g, n1_b, w3, b3, w5, b5, w7, b7, gate_w, gate_b, proj_w, proj_b, n2_g, n2_b, q_w, q_b, k_w, k_b, v_w, v_b):
        import jax, jax.numpy as jnp
        import numpy as np
        from jax import lax
        EPS = 1e-05

        def group_norm1(x, g, b):
            mu = jnp.mean(x, axis=(1, 2, 3), keepdims=True)
            var = jnp.var(x, axis=(1, 2, 3), keepdims=True)
            xn = (x - mu) * lax.rsqrt(var + EPS)
            return xn * g[None, :, None, None] + b[None, :, None, None]

        def dwconv(x, w, b):
            C = x.shape[1]
            k = w.shape[-1]
            p = k // 2
            out = lax.conv_general_dilated(x, w, (1, 1), [(p, p), (p, p)], dimension_numbers=('NCHW', 'OIHW', 'NCHW'), feature_group_count=C)
            return out + b[None, :, None, None]

        def conv1x1(x, w, b):
            return jnp.einsum('oc,bchw->bohw', w, x) + b[None, :, None, None]
        B, C, H, W = x.shape
        h = group_norm1(x, n1_g, n1_b)
        f = dwconv(h, w3, b3) + dwconv(h, w5, b5) + dwconv(h, w7, b7)
        g = jax.nn.sigmoid(conv1x1(f, gate_w, gate_b))
        x = x + conv1x1(f * g, proj_w, proj_b)
        h = group_norm1(x, n2_g, n2_b)
        N = H * W
        q = conv1x1(h, q_w, q_b).reshape(B, C, N).transpose(0, 2, 1)
        k = conv1x1(h, k_w, k_b).reshape(B, C, N)
        v = conv1x1(h, v_w, v_b).reshape(B, C, N).transpose(0, 2, 1)
        scale = C ** (-0.5)
        attn = jax.nn.softmax(jnp.einsum('bnc,bcm->bnm', q, k) * scale, axis=-1)
        out = jnp.einsum('bnm,bmc->bnc', attn, v)
        out = out.transpose(0, 2, 1).reshape(B, C, H, W)
        return x + out

    def _gn(v, G=32, eps=1e-5):
        B_, C_, H_, W_ = v.shape
        g = v.reshape(B_, G, C_ // G, H_, W_)
        m = jnp.mean(g, axis=(2, 3, 4), keepdims=True)
        s = jnp.var(g, axis=(2, 3, 4), keepdims=True)
        return ((g - m) / jnp.sqrt(s + eps)).reshape(v.shape)

    def _ln_c(v, eps=1e-6):
        m = jnp.mean(v, axis=1, keepdims=True)
        s = jnp.var(v, axis=1, keepdims=True)
        return (v - m) / jnp.sqrt(s + eps)

    def _ln_t(v, eps=1e-5):
        m = jnp.mean(v, axis=-1, keepdims=True)
        s = jnp.var(v, axis=-1, keepdims=True)
        return (v - m) / jnp.sqrt(s + eps)

    def _to_tokens(v):
        B_, C_, H_, W_ = v.shape
        return v.reshape(B_, C_, H_ * W_).transpose(0, 2, 1)
    def _from_tokens(t, like):
        B_, C_, H_, W_ = like.shape
        return t.transpose(0, 2, 1).reshape(B_, C_, H_, W_)

    x = _L0_conv_ref(x, L0_conv_n1_g, L0_conv_n1_b, L0_conv_w3, L0_conv_b3, L0_conv_w5, L0_conv_b5, L0_conv_w7, L0_conv_b7, L0_conv_gate_w, L0_conv_gate_b, L0_conv_proj_w, L0_conv_proj_b, L0_conv_n2_g, L0_conv_n2_b, L0_conv_q_w, L0_conv_q_b, L0_conv_k_w, L0_conv_k_b, L0_conv_v_w, L0_conv_v_b)
    return x


_drawn_inputs = setup_inputs


def setup_inputs(seed=0):
    import zlib

    import numpy as np

    out = dict(_drawn_inputs(seed))
    spreads = {'L0_conv_n1_g': (1.0, 0.6),
     'L0_conv_n1_b': (0.0, 0.8),
     'L0_conv_b3': (0.0, 0.365),
     'L0_conv_b5': (0.0, 0.359),
     'L0_conv_b7': (0.0, 0.417),
     'L0_conv_gate_b': (0.0, 0.8),
     'L0_conv_proj_b': (0.0, 0.1),
     'L0_conv_n2_g': (1.0, 0.6),
     'L0_conv_n2_b': (0.0, 0.1),
     'L0_conv_q_b': (0.0, 0.8),
     'L0_conv_k_b': (0.0, 0.8),
     'L0_conv_v_b': (0.0, 0.1)}
    factors = {'L0_conv_gate_w': 6.101, 'L0_conv_q_w': 5.974, 'L0_conv_k_w': 5.855}
    for name, (base, spread) in spreads.items():
        noise = np.random.default_rng([zlib.crc32(name.encode()), seed]).standard_normal(out[name].shape)
        drawn = base * np.exp(spread * noise) if base else spread * noise
        out[name] = jnp.asarray(drawn.astype(out[name].dtype))
    for name, factor in factors.items():
        out[name] = (out[name] * factor).astype(out[name].dtype)
    return out
```

```python
from contextlib import ExitStack

import numpy as np

import concourse.bass as bass
from concourse import mybir

F32 = mybir.dt.float32
F16 = mybir.dt.float16
ALU = mybir.AluOpType
ACT = mybir.ActivationFunctionType
AX = mybir.AxisListType
RMAX = bass.bass_isa.ReduceOp.max

B, C, H, W = 2, 64, 96, 96
P = 128
N = H * W
HR = H // 2
NHALF = HR * W
PAD = 3
XR = HR + 2 * PAD
HW_ = W + 2 * PAD
EPS = 1e-5

CH = 512
NCH = NHALF // CH
NBLK = N // CH
NPAIR = N // (2 * P)
NQT = CH // P
NMX = NQT * NBLK
GP = 4
NG = NPAIR // GP
NSLOT = 4
MX_OF = [2, 2, 2, 3, 2, 2, 2, 3]

TAPS = 49
DVE_TAPS = 30
PE_TAPS = TAPS - DVE_TAPS
CROWS = 4
CCH = HR // CROWS
QK_TOP = 2.0 ** 14
ONE = 2.0 ** 14
M_ROW = 1.0 / (ONE * 64)


def program(nc, x, n1_g, n1_b, w3, b3, w5, b5, w7, b7, gate_w, gate_b, proj_w, proj_b,
            n2_g, n2_b, q_w, q_b, k_w, k_b, v_w, v_b, out):
    with ExitStack() as ctx:
        def sb(name, shape, dt=F32):
            return ctx.enter_context(nc.sbuf_tensor(name, shape, dt))

        def sem(name):
            return ctx.enter_context(nc.semaphore(name))

        def flat(t):
            return t.rearrange("p a b -> p (a b)")

        x1_dram = nc.dram_tensor("x1_scratch", (B, C, N), F32, kind="Internal").ap()

        ident = sb("ident", [P, P])
        ident16 = sb("ident16", [P, P], F16)
        zero16 = sb("zero16", [P, P], F16)
        ones = sb("ones", [P, P])
        prm = sb("prm", [P, 12])
        G1, B1, G2, B2, B3, B5, B7, GB, PB, QB, KB, VB = range(12)
        w3s = sb("w3s", [P, 9])
        w5s = sb("w5s", [P, 25])
        wc = sb("wc", [P, TAPS])
        bsum = sb("bsum", [P, 1])
        wT = sb("wT", [P, 7, P])
        WG, WP, WV, WQ, WK = 0, 1, 2, 3, 5
        wstat = sb("wstat", [P, 4])
        wmax = sb("wmax", [P, 4])

        xs = sb("xs", [P, XR, W])
        hp = sb("hp", [P, XR, HW_])
        f = sb("f", [P, NHALF])
        x1 = sb("x1", [P, NHALF])
        bn = sb("bn", [P, NCH, 6])
        mv = sb("mv", [P, 2])
        tot = sb("tot", [P, 2])
        dev = sb("dev", [P, 2])
        var = sb("var", [P, 3])
        aff = sb("aff", [P, 4])
        bnd = sb("bnd", [P, 8])

        Q1 = sb("Q1", [P, N], F16)
        Q2 = sb("Q2", [P, N], F16)
        K1 = sb("K1", [P, N], F16)
        K2 = sb("K2", [P, N], F16)
        vst = sb("vst", [P, 2, 2 * GP, C])
        E = sb("E", [P, NSLOT, 2, CH])
        mxp = sb("mxp", [P, NQT, NBLK])
        m4 = sb("m4", [P, NQT])
        negm = sb("negm", [P, NQT, P], F16)
        accA = sb("accA", [P, 2, CH])
        accB = sb("accB", [P, 2, CH])
        accS = sb("accS", [P, CH])
        odd = sb("odd", [C, CH])
        rec = sb("rec", [C, CH])
        xst = sb("xst", [C, 2, CH])
        ot = sb("ot", [C, 2, CH])

        V = x1[:].rearrange("p (h t c) -> p h t c", h=2, c=C)
        T = E[:, 0:2, :, :].rearrange("p a b c -> p (a b) c")
        gs = E[:, 2, :, :]
        wnat = flat(E[:, 3, :, :])[:, 0:7 * P].rearrange("p (a b) -> p a b", a=7)
        diag = Q1[:, 0:2 * PE_TAPS * P].bitcast(F32).rearrange("p (a b) -> p a b", b=P)

        ps = ctx.enter_context(nc.psum_tensor("ps", [P, 8, CH], F32))
        S_BANK, MX_BANK, ACC_BANK = 0, 4, 6
        x_in = flat(xs[:, PAD:PAD + HR, :])

        par_in = sem("par_in")
        x_ready = sem("x_ready")
        const_ready = sem("const_ready")
        pool_step = sem("pool_step")
        dve_step = sem("dve_step")
        wc_ready = sem("wc_ready")
        diag_ready = sem("diag_ready")
        wt_ps = sem("wt_ps")
        wt_ready = sem("wt_ready")
        wmax_ready = sem("wmax_ready")
        wstat_ready = sem("wstat_ready")
        bn_done = sem("bn_done")
        m4_done = sem("m4_done")
        norm_done = sem("norm_done")
        st_in = sem("st_in")
        st_ps = sem("st_ps")
        var_ready = sem("var_ready")
        root_ready = sem("root_ready")
        aff_ready = sem("aff_ready")
        hp_act = sem("hp_act")
        hp_dve = sem("hp_dve")
        cps_ready = sem("cps_ready")
        cps_out = sem("cps_out")
        f_ready = sem("f_ready")
        gate_ready = sem("gate_ready")
        sig_ready = sem("sig_ready")
        fg_ready = sem("fg_ready")
        proj_ready = sem("proj_ready")
        x1_ready = sem("x1_ready")
        x1_stored = sem("x1_stored")
        h_ready = sem("h_ready")
        hmax_ready = sem("hmax_ready")
        hmax_all = sem("hmax_all")
        scale_ready = sem("scale_ready")
        qk_ps = sem("qk_ps")
        t_ready = sem("t_ready")
        half_ready = sem("half_ready")
        t_used = sem("t_used")
        k2_ready = sem("k2_ready")
        v_ps = sem("v_ps")
        v_out = sem("v_out")
        mx_ready = sem("mx_ready")
        mx_free = sem("mx_free")
        nm_ready = sem("nm_ready")
        mb_ready = sem("mb_ready")
        m_ready = sem("m_ready")
        s_ready = sem("s_ready")
        e_ready = sem("e_ready")
        pv_free = sem("pv_free")
        adda_free = sem("adda_free")
        addb_free = sem("addb_free")
        vst_ready = [sem("vst_ready0"), sem("vst_ready1")]
        zero_a = sem("zero_a")
        zero_b = sem("zero_b")
        sum_ready = sem("sum_ready")
        rs_ready = sem("rs_ready")
        rs_used = sem("rs_used")
        odd_ready = sem("odd_ready")
        acc_free = sem("acc_free")
        xst_ready = [sem("xst_ready0"), sem("xst_ready1")]
        o_ready = sem("o_ready")
        o_stored = [sem("o_stored0"), sem("o_stored1")]

        PER_HALF = [(n1_g, G1), (n1_b, B1), (n2_g, G2), (n2_b, B2), (b3, B3), (b5, B5), (b7, B7),
                    (gate_b, GB), (proj_b, PB), (q_b, QB), (k_b, KB), (v_b, VB)]
        TAP_LOADS = [(w3, w3s), (w5, w5s), (w7, wc)]
        MAT_LOADS = [(gate_w, WG, 0, 0), (gate_w, WG, 1, 1), (proj_w, WP, 0, 0), (proj_w, WP, 1, 1),
                     (v_w, WV, 0, 0), (v_w, WV, 1, 1)]
        MAT_LOADS += [(w, i + h, dup, h) for w, i in ((q_w, WQ), (k_w, WK)) for h in (0, 1) for dup in (0, 1)]
        N_PAR = 2 * len(PER_HALF) + 2 * len(TAP_LOADS) + len(MAT_LOADS)

        def taps(t):
            dy, dx = divmod(t, 7)
            return dy, dx

        def window(t, r0, rows):
            dy, dx = taps(t)
            return hp[:, r0 + dy:r0 + dy + rows, dx:dx + W]

        def blk(b, j):
            return NBLK * b + j

        def pair0(b, j):
            return NPAIR * blk(b, j)

        block = ctx.enter_context(nc.Block())

        @block.sync
        def _(sp):
            def load_x(b):
                for h in (0, 1):
                    r = 0 if h == 0 else HR - PAD
                    to = PAD if h == 0 else 0
                    sp.dma_start(xs[C * h:C * h + C, to:to + HR + PAD, :],
                                 x[b, :, r:r + HR + PAD, :]).then_inc(x_ready, 16)

            for par in (0, 1):
                sp.sem_inc(o_stored[par], 16)
            load_x(0)
            sp.wait_ge(const_ready, 2)
            for w, i, rh, ch in MAT_LOADS:
                sp.dma_start(wnat[C * rh:C * rh + C, i, C * ch:C * ch + C], w[:, :]).then_inc(par_in, 16)

            def load_v(b, j, par, d, gg):
                g = 2 * gg + d
                n = blk(b, j) * NG + g
                slot = (par + d) % 2
                if not (isinstance(n, int) and n < 2):
                    sp.wait_ge(pv_free, GP * n)
                sp.dma_start(flat(vst[:, slot, :, :]), x1[:, bass.ds(g * (2 * GP * C), 2 * GP * C)]
                             ).then_inc(vst_ready[slot], 16)

            def attend(b, j, par, store):
                if b == 0 and isinstance(j, int) and j == 0:
                    for g in range(NG - 1):
                        load_v(b, j, par, g % 2, g // 2)
                else:
                    with sp.Fori(0, NG // 2) as gg:
                        for d in (0, 1):
                            load_v(b, j, par, d, gg)
                load_v(b, j, par, 0, NG // 2)
                if not (b == 0 and isinstance(j, int) and j < 2):
                    sp.wait_ge(o_ready, blk(b, j))
                sp.dma_start(xst[:, par, :], x1_dram[b, :, bass.ds(j * CH, CH)]).then_inc(xst_ready[par], 16)
                if store:
                    store_out(b, j - 2, par)

            def store_out(b, j, par):
                sp.wait_ge(o_ready, blk(b, j) + 2)
                sp.dma_start(out[b, :, bass.ds(j * CH, CH)], ot[:, par, :]).then_inc(o_stored[par], 16)

            for b in range(B):
                sp.wait_ge(x1_ready, NCH * (b + 1))
                for h in (0, 1):
                    sp.dma_start(x1_dram[b, :, h * NHALF:(h + 1) * NHALF], x1[C * h:C * h + C, :]).then_inc(x1_stored, 16)
                if b + 1 < B:
                    load_x(b + 1)
                sp.wait_ge(x1_stored, 32 * (b + 1))
                sp.wait_ge(v_out, NCH * (b + 1))
                attend(b, 0, 0, False)
                attend(b, 1, 1, False)
                with sp.Fori(1, NBLK // 2) as jj:
                    for par in (0, 1):
                        attend(b, 2 * jj + par, par, True)
                store_out(b, NBLK - 2, 0)
                store_out(b, NBLK - 1, 1)
            for par in (0, 1):
                sp.wait_ge(o_stored[par], 16 * B * NBLK // 2 + 16)

        @block.gpsimd
        def _(pool):
            nc.gpsimd.memset(ident[:], 0.0).then_inc(pool_step, 1)
            nc.gpsimd.memset(ones[:], 1.0).then_inc(const_ready, 1)
            nc.gpsimd.memset(flat(wnat), 0.0).then_inc(const_ready, 1)
            pool.wait_ge(pool_step, 1)
            nc.gpsimd.affine_select(out=ident[:], in_=ident[:], compare_op=ALU.not_equal, fill=1.0, base=0,
                                    pattern=[[-1, P]], channel_multiplier=1).then_inc(const_ready, 1)
            nc.gpsimd.memset(zero16[:], 0.0).then_inc(const_ready, 1)
            nc.gpsimd.sem_inc(adda_free, NSLOT)
            pool.wait_ge(wstat_ready, 1)
            nc.gpsimd.partition_all_reduce(wmax[:], wstat[:], P, RMAX).then_inc(wmax_ready, 1)

            def total(b, j, par):
                pool.wait_ge(addb_free, NSLOT + pair0(b, j) + NPAIR)
                pool.wait_ge(adda_free, NSLOT + pair0(b, j) + NPAIR)
                pool.wait_ge(rs_ready, blk(b, j) + 1)
                nc.gpsimd.tensor_tensor(accS[:], accA[:, par, :], accB[:, par, :], ALU.add).then_inc(sum_ready, 1)

            def attend(b, j, par, first=False, last=False):
                with pool.Fori(0, NG // 2) as gg:
                    for p in range(2 * GP):
                        add_a(b, j, par, (2 * GP * gg, p))
                for p in range(GP):
                    if p == 0 and not first:
                        total(b, j - 1, 1 - par)
                    if p == 1 and not first:
                        pool.wait_ge(sum_ready, blk(b, j))
                    add_a(b, j, par, (NPAIR - GP, p))
                    if p == 1 and not last:
                        nc.gpsimd.memset(accA[:, 1 - par, :], 0.0).then_inc(zero_a, 1)
                    if p == 2 and not last:
                        pool.wait_ge(zero_a, blk(b, j) + 2)

            def add_a(b, j, par, i):
                n = pair0(b, j) + i[0] + i[1]
                pool.wait_ge(e_ready, n + 2)
                pool.wait_ge(adda_free, NSLOT + n)
                nc.gpsimd.tensor_tensor(accA[:, par, :], accA[:, par, :], E[:, i[1] % NSLOT, 0, :], ALU.add
                                        ).then_inc(adda_free, 1)

            for b in range(B):
                pool.wait_ge(hmax_ready, b + 1)
                nc.gpsimd.partition_all_reduce(bnd[:, 1:2], bnd[:, 0:1], P, RMAX).then_inc(hmax_all, 1)
                if b:
                    pool.wait_ge(sum_ready, blk(b, 0))
                nc.gpsimd.memset(accA[:, 0, :], 0.0).then_inc(zero_a, 1)
                pool.wait_ge(zero_a, blk(b, 0) + 1)
                attend(b, 0, 0, first=True)
                with pool.Fori(0, (NBLK - 2) // 2) as jj:
                    attend(b, 2 * jj + 1, 1)
                    attend(b, 2 * jj + 2, 0)
                attend(b, NBLK - 1, 1, last=True)
                total(b, NBLK - 1, 1)

        @block.scalar
        def _(act):
            act.sem_inc(e_ready, 1)
            for src, dst in TAP_LOADS:
                for h in (0, 1):
                    act.dma_start(dst[C * h:C * h + C, :], src.rearrange("c a y x -> c (a y x)")).then_inc(par_in, 16)
            for src, i in PER_HALF:
                for h in (0, 1):
                    act.dma_start(prm[C * h:C * h + C, i:i + 1], src.rearrange("(c a) -> c a", a=1)).then_inc(par_in, 16)
            def exponentials(b, j, i):
                n = pair0(b, j) + i[0] + i[1]
                slot, buf = i[1] % NSLOT, i[1] % 2
                act.wait_ge(s_ready, n + 1)
                act.wait_ge(pv_free, n + 1)
                act.wait_ge(adda_free, n + 1)
                act.wait_ge(addb_free, n + 1)
                nc.scalar.activation(flat(E[:, slot, :, :]), flat(ps[:, S_BANK + 2 * buf:S_BANK + 2 * buf + 2, :]),
                                     ACT.Exp, scale=bnd[:, 6:7]).then_inc(e_ready, 1)

            def move_odd(b, j, par):
                act.wait_ge(pv_free, NSLOT + pair0(b, j) + NPAIR)
                act.wait_ge(o_ready, blk(b, j) + 1)
                nc.scalar.activation(odd[:], ps[C:P, ACC_BANK + par, :], ACT.Copy).then_inc(odd_ready, 1)

            def attend(b, j, par, first=False):
                with act.Fori(0, NG // 2) as gg:
                    for p in range(2 * GP):
                        exponentials(b, j, (2 * GP * gg, p))
                for p in range(GP):
                    exponentials(b, j, (NPAIR - GP, p))
                    if p == 0 and not first:
                        move_odd(b, j - 1, 1 - par)

            def diagonals():
                for t in range(PE_TAPS):
                    a = nc.scalar.activation(diag[:, t, :], ident[:], ACT.Copy,
                                             scale=wc[:, DVE_TAPS + t:DVE_TAPS + t + 1])
                a.then_inc(diag_ready, 1)

            act.wait_ge(const_ready, 3)
            act.wait_ge(wc_ready, 1)
            diagonals()
            def root(n):
                act.wait_ge(var_ready, n + 1)
                nc.scalar.activation(var[:, 1:2], var[:, 0:1], ACT.Sqrt).then_inc(root_ready, 1)

            for b in range(B):
                root(2 * b)
                act.wait_ge(aff_ready, 2 * b + 1)
                if b:
                    diagonals()
                nc.scalar.activation(hp[0:C, PAD:XR, PAD:PAD + W], xs[0:C, PAD:XR, :], ACT.Identity,
                                     bias=aff[0:C, 1:2], scale=aff[0:C, 0:1]).then_inc(hp_act, 1)
                for c in range(CCH):
                    n = CCH * b + c
                    act.wait_ge(cps_ready, n + 1)
                    nc.scalar.activation(x1[:, c * CROWS * W:(c + 1) * CROWS * W],
                                         ps[:, c % 4, 0:CROWS * W], ACT.Copy).then_inc(cps_out, 1)
                for c in range(NCH):
                    n = NCH * b + c
                    act.wait_ge(gate_ready, n + 1)
                    if c >= 2:
                        act.wait_ge(fg_ready, n - 1)
                    nc.scalar.activation(gs[:, c % 2, :], ps[:, c % 2, :], ACT.Sigmoid,
                                         bias=prm[:, GB:GB + 1]).then_inc(sig_ready, 1)
                root(2 * b + 1)
                act.wait_ge(aff_ready, 2 * b + 2)
                nc.scalar.activation(f[:], x1[:], ACT.Identity, bias=aff[:, 3:4], scale=aff[:, 2:3]).then_inc(h_ready, 1)
                act.wait_ge(scale_ready, b + 1)
                for c in range(2 * NCH):
                    for k in (0, 1):
                        e = 2 * c + k
                        n = 4 * NCH * b + e
                        act.wait_ge(qk_ps, n + 1)
                        if n >= 4:
                            act.wait_ge(t_used, n - 3)
                        nc.scalar.activation(T[:, e % 4, :], ps[:, e % 4, :], ACT.Identity,
                                             bias=bnd[:, 4 + k:5 + k], scale=bnd[:, 2 + k:3 + k]).then_inc(t_ready, 1)
                    act.wait_ge(half_ready, 4 * NCH * b + 2 * c + 2)
                    nc.scalar.activation(K2[0:C, c * CH:(c + 1) * CH], K1[0:C, c * CH:(c + 1) * CH], ACT.Copy).then_inc(k2_ready, 1)
                attend(b, 0, 0, first=True)
                with act.Fori(0, (NBLK - 2) // 2) as jj:
                    attend(b, 2 * jj + 1, 1)
                    attend(b, 2 * jj + 2, 0)
                attend(b, NBLK - 1, 1)
                move_odd(b, NBLK - 1, 1)

        @block.vector
        def _(dve):
            steps = [0]

            def chain(ins):
                steps[0] += 1
                ins.then_inc(dve_step, 1)
                dve.wait_ge(dve_step, steps[0])

            nc.vector.memset(hp[:].rearrange("p a b -> p (a b)"), 0.0).then_inc(dve_step, 1)
            steps[0] += 1
            dve.sem_inc(acc_free, 2)
            dve.sem_inc(rs_used, 1)
            dve.sem_inc(o_ready, 1)
            dve.sem_inc(mx_free, 2)
            dve.sem_inc(addb_free, NSLOT)
            dve.wait_ge(const_ready, 3)
            nc.vector.tensor_copy(ident16[:], ident[:]).then_inc(const_ready, 1)
            nc.vector.memset(K2[C:P, :], ONE).then_inc(const_ready, 1)
            dve.wait_ge(par_in, 16 * N_PAR)
            for k, src in ((5, w5s), (3, w3s)):
                o = (7 - k) // 2
                mid = wc[:].rearrange("p (y x) -> p y x", x=7)[:, o:o + k, o:o + k]
                chain(nc.vector.tensor_tensor(mid, mid, src[:].rearrange("p (y x) -> p y x", x=k), ALU.add))
            chain(nc.vector.tensor_tensor(bsum[:], prm[:, B3:B3 + 1], prm[:, B5:B5 + 1], ALU.add))
            nc.vector.tensor_tensor(bsum[:], bsum[:], prm[:, B7:B7 + 1], ALU.add).then_inc(wc_ready, 1)
            for k, w, bias in ((0, WQ, QB), (1, WK, KB)):
                nc.vector.tensor_reduce(wstat[:, k:k + 1], wnat[:, w, :], AX.X, ALU.add, apply_absolute_value=True)
                last = nc.vector.tensor_reduce(wstat[:, 2 + k:3 + k], prm[:, bias:bias + 1], AX.X, ALU.max,
                                               apply_absolute_value=True)
            last.then_inc(wstat_ready, 1)
            dve.wait_ge(wt_ps, 1)
            nc.vector.tensor_copy(wT[:, 0:4, :].rearrange("p a b -> p (a b)"), ps[:, 0, :])
            nc.vector.tensor_copy(wT[:, 4:7, :].rearrange("p a b -> p (a b)"), ps[:, 1, 0:3 * P]).then_inc(wt_ready, 1)

            def norm(b, second, gamma, beta, col):
                dve.wait_ge(bn_done, NCH * (2 * b + second + 1))
                nc.vector.bn_aggr(mv[:], bn[:].rearrange("p a b -> p (a b)")).then_inc(st_in, 1)
                dve.wait_ge(st_ps, 4 * b + 2 * second + 1)
                chain(nc.vector.tensor_scalar(tot[:], ps[:, 7, 0:2], 1.0 / P, None, ALU.mult))
                chain(nc.vector.tensor_tensor(dev[:, 0:1], mv[:, 0:1], tot[:, 0:1], ALU.subtract))
                nc.vector.tensor_tensor(dev[:, 1:2], dev[:, 0:1], dev[:, 0:1], ALU.mult).then_inc(st_in, 1)
                dve.wait_ge(st_ps, 4 * b + 2 * second + 2)
                chain(nc.vector.scalar_tensor_tensor(out=tot[:, 1:2], in0=ps[:, 7, 2:3], scalar=1.0 / P,
                                                     in1=tot[:, 1:2], op0=ALU.mult, op1=ALU.add))
                nc.vector.tensor_scalar(var[:, 0:1], tot[:, 1:2], EPS, None, ALU.add).then_inc(var_ready, 1)
                dve.wait_ge(root_ready, 2 * b + second + 1)
                chain(nc.vector.reciprocal(tot[:, 1:2], var[:, 1:2]))
                chain(nc.vector.tensor_tensor(var[:, 2:3], tot[:, 1:2], tot[:, 1:2], ALU.mult))
                chain(nc.vector.tensor_tensor(var[:, 2:3], var[:, 2:3], var[:, 0:1], ALU.mult))
                chain(nc.vector.tensor_scalar(var[:, 2:3], var[:, 2:3], -0.5, 1.5, ALU.mult, ALU.add))
                chain(nc.vector.tensor_tensor(tot[:, 1:2], tot[:, 1:2], var[:, 2:3], ALU.mult))
                chain(nc.vector.tensor_tensor(aff[:, col:col + 1], prm[:, gamma:gamma + 1], tot[:, 1:2], ALU.mult))
                chain(nc.vector.tensor_tensor(tot[:, 0:1], tot[:, 0:1], aff[:, col:col + 1], ALU.mult))
                nc.vector.tensor_tensor(aff[:, col + 1:col + 2], prm[:, beta:beta + 1], tot[:, 0:1],
                                        ALU.subtract).then_inc(aff_ready, 1)

            def reduce_max(m, at, c):
                dve.wait_ge(mx_ready, m + 1)
                nc.vector.reduce_max(at, ps[:, MX_BANK + c % 2, :], AX.X).then_inc(mx_free, 1)

            def maxima(b, j):
                f0 = blk(b, j)
                dve.wait_ge(mx_free, 2 + NMX * (f0 + 1))
                nc.vector.reduce_max(m4[:], mxp[:], AX.X).then_inc(m4_done, 1)
                dve.wait_ge(m4_done, f0 + 1)
                dve.wait_ge(mb_ready, f0)
                nc.vector.tensor_scalar(negm[:], m4[:].unsqueeze(2).to_broadcast([P, NQT, P]), -M_ROW, None,
                                        ALU.mult).then_inc(nm_ready, 1)
                dve.wait_ge(mb_ready, f0 + 1)
                nc.vector.tensor_copy(Q2[C:P, bass.ds(j * CH, CH)], ps[C:P, MX_BANK, :]).then_inc(m_ready, 1)

            def add_b(b, j, par, i):
                n = pair0(b, j) + i[0] + i[1]
                dve.wait_ge(e_ready, n + 2)
                dve.wait_ge(addb_free, NSLOT + n)
                nc.vector.tensor_tensor(accB[:, par, :], accB[:, par, :], E[:, i[1] % NSLOT, 1, :], ALU.add
                                        ).then_inc(addb_free, 1)

            def attend(b, j, par, first=False, last=False, jhalf=None):
                n0 = pair0(b, j)
                m0 = NMX * (blk(b, j) + 1)
                with dve.Fori(0, NG // 2) as gg:
                    c = 0
                    for p in range(2 * GP):
                        if not last:
                            for _ in range(MX_OF[p]):
                                reduce_max(m0 + NBLK * gg + c, mxp_at(gg, c), c)
                                c += 1
                        add_b(b, j, par, (2 * GP * gg, p))
                if not last:
                    maxima(b, j + 1)
                for p in range(GP):
                    if p == 2 and not last:
                        dve.wait_ge(zero_b, blk(b, j) + 2)
                    add_b(b, j, par, (NPAIR - GP, p))
                    if p == 1 and not first:
                        finish(b, j - 1, 1 - par, jhalf)
                    if p == 1 and not last:
                        dve.wait_ge(sum_ready, blk(b, j))
                        nc.vector.memset(accB[:, 1 - par, :], 0.0).then_inc(zero_b, 1)

            def mxp_at(gg, c):
                return flat(mxp[:])[:, bass.ds(NBLK * gg + c, 1)]

            def finish(b, j, par, jhalf):
                f0 = blk(b, j)
                done = (b * (NBLK // 2) + (j // 2 if jhalf is None else jhalf)) * 16
                dve.wait_ge(odd_ready, f0 + 1)
                nc.vector.tensor_tensor(odd[:], ps[0:C, ACC_BANK + par, :], odd[:], ALU.add).then_inc(acc_free, 1)
                dve.wait_ge(rs_ready, f0 + 2)
                nc.vector.reciprocal(rec[:], ps[0:C, MX_BANK + 1, :]).then_inc(rs_used, 1)
                dve.wait_ge(acc_free, f0 + 3)
                dve.wait_ge(rs_used, f0 + 2)
                nc.vector.tensor_tensor(odd[:], odd[:], rec[:], ALU.mult).then_inc(norm_done, 1)
                dve.wait_ge(norm_done, f0 + 1)
                dve.wait_ge(xst_ready[par], done + 16)
                dve.wait_ge(o_stored[par], done + 16)
                nc.vector.scalar_tensor_tensor(out=ot[:, par, :], in0=odd[:], scalar=prm[0:C, VB:VB + 1],
                                               in1=xst[:, par, :], op0=ALU.add, op1=ALU.add).then_inc(o_ready, 1)

            for b in range(B):
                dve.wait_ge(x_ready, 32 * (b + 1))
                for c in range(NCH):
                    nc.vector.bn_stats(bn[:, c, :], x_in[:, c * CH:(c + 1) * CH]).then_inc(bn_done, 1)
                norm(b, 0, G1, B1, 0)
                dve.wait_ge(aff_ready, 2 * b + 1)
                nc.vector.tensor_scalar(hp[C:P, 0:HR + PAD, PAD:PAD + W], xs[C:P, 0:HR + PAD, :], aff[C:P, 0:1],
                                        aff[C:P, 1:2], ALU.mult, ALU.add).then_inc(hp_dve, 1)
                dve.wait_ge(hp_act, b + 1)
                dve.wait_ge(hp_dve, b + 1)
                f3 = f[:].rearrange("p (y x) -> p y x", x=W)
                chain(nc.vector.tensor_scalar(f3, window(0, 0, HR), wc[:, 0:1], bsum[:], ALU.mult, ALU.add))
                for t in range(1, DVE_TAPS):
                    chain(nc.vector.scalar_tensor_tensor(out=f3, in0=window(t, 0, HR), scalar=wc[:, t:t + 1], in1=f3,
                                                         op0=ALU.mult, op1=ALU.add))
                dve.wait_ge(cps_out, CCH * (b + 1))
                nc.vector.tensor_tensor(f[:], f[:], x1[:], ALU.add).then_inc(f_ready, 1)
                dve.wait_ge(f_ready, b + 1)

                def gated(c):
                    dve.wait_ge(sig_ready, NCH * b + c + 1)
                    at = f[:, c * CH:(c + 1) * CH]
                    nc.vector.tensor_tensor(at, at, gs[:, c % 2, :], ALU.mult).then_inc(fg_ready, 1)

                gated(0)
                for c in range(NCH):
                    n = NCH * b + c
                    if c + 1 < NCH:
                        gated(c + 1)
                    dve.wait_ge(proj_ready, n + 1)
                    at = x1[:, c * CH:(c + 1) * CH]
                    nc.vector.scalar_tensor_tensor(out=at, in0=ps[:, 2 + c % 2, :], scalar=prm[:, PB:PB + 1],
                                                   in1=x_in[:, c * CH:(c + 1) * CH], op0=ALU.add,
                                                   op1=ALU.add).then_inc(x1_ready, 1)
                    dve.wait_ge(x1_ready, n + 1)
                    nc.vector.bn_stats(bn[:, c, :], at).then_inc(bn_done, 1)
                norm(b, 1, G2, B2, 2)
                dve.wait_ge(h_ready, b + 1)
                nc.vector.tensor_reduce(bnd[:, 0:1], f[:], AX.X, ALU.max, apply_absolute_value=True).then_inc(hmax_ready, 1)
                dve.wait_ge(hmax_all, b + 1)
                dve.wait_ge(wmax_ready, 1)
                chain(nc.vector.scalar_tensor_tensor(out=bnd[:, 4:6], in0=wmax[:, 0:2], scalar=bnd[:, 1:2],
                                                     in1=wmax[:, 2:4], op0=ALU.mult, op1=ALU.add))
                chain(nc.vector.tensor_scalar(bnd[:, 4:6], bnd[:, 4:6], 1e-12, 1.0 / QK_TOP, ALU.max, ALU.mult))
                chain(nc.vector.reciprocal(bnd[:, 2:4], bnd[:, 4:6]))
                chain(nc.vector.tensor_tensor(bnd[:, 6:7], bnd[:, 4:5], bnd[:, 5:6], ALU.mult))
                chain(nc.vector.tensor_scalar(bnd[:, 6:7], bnd[:, 6:7], C ** -0.5, None, ALU.mult))
                nc.vector.tensor_tensor(bnd[:, 4:6], bnd[:, 2:4], prm[:, QB:QB + 2], ALU.mult).then_inc(scale_ready, 1)
                for c in range(2 * NCH):
                    cols = slice(c * CH, (c + 1) * CH)
                    for k, whole, low, rows in ((0, Q1, Q2, slice(0, C)), (1, K1, K1, slice(C, P))):
                        e = 2 * c + k
                        n = 4 * NCH * b + e
                        dve.wait_ge(t_ready, n + 1)
                        nc.vector.tensor_copy(whole[:, cols], T[:, e % 4, :]).then_inc(half_ready, 1)
                        dve.wait_ge(half_ready, n + 1)
                        nc.vector.tensor_tensor(low[rows, cols], T[rows, e % 4, :], whole[rows, cols],
                                                ALU.subtract).then_inc(t_used, 1)
                dve.wait_ge(x1_stored, 32 * (b + 1))
                for g in range(NCH):
                    for q in range(8):
                        c = 8 * g + q
                        reduce_max(NMX * blk(b, 0) + c, flat(mxp[:])[:, c:c + 1], c)
                    dve.wait_ge(v_ps, NCH * b + g + 1)
                    nc.vector.tensor_copy(V[:, :, NQT * g:NQT * g + NQT, :].rearrange("p h t c -> p t h c"),
                                          ps[:, ACC_BANK + g % 2, :].rearrange("p (t h c) -> p t h c", t=NQT, h=2)
                                          ).then_inc(v_out, 1)
                maxima(b, 0)
                if b:
                    dve.wait_ge(sum_ready, blk(b, 0))
                nc.vector.memset(accB[:, 0, :], 0.0).then_inc(zero_b, 1)
                dve.wait_ge(zero_b, blk(b, 0) + 1)
                attend(b, 0, 0, first=True)
                with dve.Fori(0, (NBLK - 2) // 2) as jj:
                    attend(b, 2 * jj + 1, 1, jhalf=jj)
                    attend(b, 2 * jj + 2, 0, jhalf=jj)
                attend(b, NBLK - 1, 1, last=True)
                finish(b, NBLK - 1, 1, None)

        @block.tensor
        def _(pe):
            pe.sem_inc(rs_ready, 1)
            pe.sem_inc(pv_free, NSLOT)
            pe.wait_ge(const_ready, 6)
            pe.wait_ge(par_in, 16 * N_PAR)
            for i in range(7):
                a = nc.tensor.transpose(ps[:, i // 4, (i % 4) * P:(i % 4 + 1) * P], wnat[:, i, :], ident[:])
            a.then_inc(wt_ps, 1)
            pe.wait_ge(wt_ready, 1)

            def stats(n):
                pe.wait_ge(st_in, n + 1)
                nc.tensor.matmul(ps[:, 7, 0:2], ones[:], mv[:], start=True, stop=True).then_inc(st_ps, 1)
                pe.wait_ge(st_in, n + 2)
                nc.tensor.matmul(ps[:, 7, 2:3], ones[:], dev[:, 1:2], start=True, stop=True).then_inc(st_ps, 1)

            def scores(b, j, i, n, peers):
                base, p = i
                buf = p % 2
                if peers is not None:
                    pe.wait_ge(e_ready, peers + 1)
                for t in (0, 1):
                    k = bass.ds((base + p) * 2 * P + t * P, P)
                    dst = ps[:, S_BANK + 2 * buf + t, :]
                    nc.tensor.matmul(dst, K1[:, k], Q1[:, bass.ds(j * CH, CH)], start=True, stop=False)
                    a = nc.tensor.matmul(dst, K2[:, k], Q2[:, bass.ds(j * CH, CH)], start=False, stop=True)
                a.then_inc(s_ready, 1)

            def weigh(b, par, p, n, slot):
                pe.wait_ge(e_ready, n + 2)
                for t in (0, 1):
                    a = nc.tensor.matmul(ps[C * t:C * t + C, ACC_BANK + par, :], vst[:, slot, 2 * (p % GP) + t, :],
                                         E[:, p % NSLOT, t, :], start=False, stop=False, skip_group_check=True)
                a.then_inc(pv_free, 1)

            def max_scores(j, qt, m, c):
                pe.wait_ge(mx_free, m + 1)
                nc.tensor.matmul(ps[:, MX_BANK + c % 2, :], Q1[:, bass.ds(j * CH + qt * P, P)],
                                 K1[:, (c % NBLK) * CH:(c % NBLK + 1) * CH], start=True, stop=True).then_inc(mx_ready, 1)

            def spread_maxima(b, j):
                pe.wait_ge(nm_ready, blk(b, j) + 1)
                for q in range(NQT):
                    a = nc.tensor.matmul(ps[:, MX_BANK, q * P:(q + 1) * P], negm[:, q, :], ident16[:], start=True, stop=True)
                a.then_inc(mb_ready, 1)

            def row_sums(b, j):
                pe.wait_ge(sum_ready, blk(b, j) + 1)
                nc.tensor.matmul(ps[0:C, MX_BANK + 1, :], ones[:, 0:C], accS[:], start=True, stop=True).then_inc(rs_ready, 1)

            def vst_wait(b, j, par, jhalf, d, gg):
                slot = (par + d) % 2
                n = NG * (blk(b, 0) // 2) + NG * jhalf + (NG * par + d) // 2 + gg
                pe.wait_ge(vst_ready[slot], 16 * (n + 1))
                return slot

            def attend(b, j, par, jhalf, first=False, last=False):
                n0 = pair0(b, j)
                m0 = NMX * (blk(b, j) + 1)
                pe.wait_ge(acc_free, blk(b, j) + 1)
                if not first:
                    pe.wait_ge(rs_used, blk(b, j))
                nc.tensor.matmul(ps[:, ACC_BANK + par, :], zero16[:], Q1[:, 0:CH], start=True, stop=True)
                with pe.Fori(0, NG // 2) as gg:
                    c = 0
                    for p in range(2 * GP):
                        n = n0 + 2 * GP * gg + p
                        scores(b, j, (2 * GP * gg, p + 1), n + 1, n)
                        if not last:
                            for _ in range(MX_OF[p]):
                                max_scores(j + 1, gg, m0 + NBLK * gg + c, c)
                                c += 1
                        if p % GP == 0:
                            slot = vst_wait(b, j, par, jhalf, p // GP, gg)
                        weigh(b, par, p, n, slot)
                slot = vst_wait(b, j, par, jhalf, NG - 1, 0)
                for p in range(GP):
                    n = n0 + NPAIR - GP + p
                    if p < GP - 1:
                        scores(b, j, (NPAIR - GP, p + 1), n + 1, n)
                    elif not last:
                        pe.wait_ge(m_ready, blk(b, j) + 2)
                        scores(b, j + 1, (0, 0), n + 1, n)
                    if p == 1 and not last:
                        spread_maxima(b, j + 1)
                    if p == 1 and not first:
                        row_sums(b, j - 1)
                    weigh(b, par, p, n, slot)

            for b in range(B):
                if b:
                    pe.wait_ge(o_ready, NBLK * b + 1)
                stats(4 * b)
                pe.wait_ge(diag_ready, b + 1)
                pe.wait_ge(hp_act, b + 1)
                pe.wait_ge(hp_dve, b + 1)
                for c in range(CCH):
                    n = CCH * b + c
                    if c >= 4:
                        pe.wait_ge(cps_out, n - 3)
                    for t in range(PE_TAPS):
                        a = nc.tensor.matmul(ps[:, c % 4, 0:CROWS * W].rearrange("p (y x) -> p y x", x=W),
                                             diag[:, t, :], window(DVE_TAPS + t, c * CROWS, CROWS),
                                             start=(t == 0), stop=(t == PE_TAPS - 1))
                    a.then_inc(cps_ready, 1)

                def gate(c):
                    n = NCH * b + c
                    if c >= 2:
                        pe.wait_ge(sig_ready, n - 1)
                    nc.tensor.matmul(ps[:, c % 2, :], wT[:, WG, :], f[:, c * CH:(c + 1) * CH], start=True,
                                     stop=True).then_inc(gate_ready, 1)

                pe.wait_ge(f_ready, b + 1)
                gate(0)
                for c in range(NCH):
                    n = NCH * b + c
                    if c + 1 < NCH:
                        gate(c + 1)
                    pe.wait_ge(fg_ready, n + 1)
                    if c >= 2:
                        pe.wait_ge(x1_ready, n - 1)
                    nc.tensor.matmul(ps[:, 2 + c % 2, :], wT[:, WP, :], f[:, c * CH:(c + 1) * CH], start=True,
                                     stop=True).then_inc(proj_ready, 1)
                stats(4 * b + 2)
                pe.wait_ge(h_ready, b + 1)
                for c in range(2 * NCH):
                    h, cc = divmod(c, NCH)
                    for k, w in ((0, WQ + h), (1, WK + h)):
                        e = 2 * c + k
                        n = 4 * NCH * b + e
                        if e >= 4:
                            pe.wait_ge(t_ready, n - 3)
                        nc.tensor.matmul(ps[:, e % 4, :], wT[:, w, :], f[:, cc * CH:(cc + 1) * CH], start=True,
                                         stop=True).then_inc(qk_ps, 1)
                pe.wait_ge(t_used, 4 * NCH * (b + 1))
                for g in range(NCH):
                    if g >= 2:
                        pe.wait_ge(v_out, NCH * b + g - 1)
                    for q in range(8):
                        c = 8 * g + q
                        max_scores(0, c // NBLK, NMX * blk(b, 0) + c, c)
                        if q % 2:
                            t = NQT * g + q // 2
                            a = nc.tensor.matmul(ps[:, ACC_BANK + g % 2, (q // 2) * P:(q // 2 + 1) * P],
                                                 f[:, t * P:(t + 1) * P], wT[:, WV, :], start=True, stop=True)
                    a.then_inc(v_ps, 1)
                spread_maxima(b, 0)
                pe.wait_ge(k2_ready, 2 * NCH * (b + 1))
                pe.wait_ge(v_out, NCH * (b + 1))
                pe.wait_ge(m_ready, blk(b, 0) + 1)
                scores(b, 0, (0, 0), pair0(b, 0), None)
                attend(b, 0, 0, 0, first=True)
                with pe.Fori(0, (NBLK - 2) // 2) as jj:
                    attend(b, 2 * jj + 1, 1, jj)
                    attend(b, 2 * jj + 2, 0, jj + 1)
                attend(b, NBLK - 1, 1, NBLK // 2 - 1, last=True)
                row_sums(b, NBLK - 1)


_INS = ['x', 'L0_conv_n1_g', 'L0_conv_n1_b', 'L0_conv_w3', 'L0_conv_b3', 'L0_conv_w5', 'L0_conv_b5',
        'L0_conv_w7', 'L0_conv_b7', 'L0_conv_gate_w', 'L0_conv_gate_b', 'L0_conv_proj_w', 'L0_conv_proj_b',
        'L0_conv_n2_g', 'L0_conv_n2_b', 'L0_conv_q_w', 'L0_conv_q_b', 'L0_conv_k_w', 'L0_conv_k_b',
        'L0_conv_v_w', 'L0_conv_v_b']


def kernel(**inputs):
    import concourse.bacc as bacc
    from concourse.bass_utils import run_bass_kernel_spmd

    nc = bacc.Bacc("TRN2", target_bir_lowering=False, num_devices=1)
    arrays, args = {}, []
    for name in _INS:
        a = np.ascontiguousarray(inputs[name])
        arrays[f"in_{name}"] = a
        args.append(nc.dram_tensor(f"in_{name}", a.shape, mybir.dt.from_np(a.dtype), kind="ExternalInput").ap())
    out = nc.dram_tensor("out", (B, C, N), F32, kind="ExternalOutput").ap()
    program(nc, *args, out)
    r = run_bass_kernel_spmd(nc, [arrays], core_ids=[0])
    return r.results[0]["out"].reshape(B, C, H, W)
```

```python
from contextlib import ExitStack

import numpy as np

import concourse.bass as bass
from concourse import mybir

F32 = mybir.dt.float32
F16 = mybir.dt.float16
ALU = mybir.AluOpType
ACT = mybir.ActivationFunctionType
AX = mybir.AxisListType
RMAX = bass.bass_isa.ReduceOp.max

B, C, H, W = 2, 64, 96, 96
P = 128
N = H * W
HR = H // 2
NHALF = HR * W
PAD = 3
XR = HR + 2 * PAD
HW_ = W + 2 * PAD
EPS = 1e-5

CH = 512
HCH = CH // 2
NCH = NHALF // CH
NBLK = N // CH
NPAIR = N // (2 * P)
NQT = CH // P
NMX = NQT * NBLK
GP = 4
NG = NPAIR // GP
STRIPS = 8
SROWS = HR // STRIPS
NSLOT = GP
POOL_ADDS, DVE_ADDS = GP + 1, GP - 1

TAPS = 49
N_PRM = 11 + 9 + 25 + TAPS
DVE_TAPS = 30
PE_TAPS = TAPS - DVE_TAPS
CROWS = 4
CCH = HR // CROWS
QK_TOP = 2.0 ** 14
ONE = 2.0 ** 14
M_ROW = 1.0 / (ONE * 64)


def program(nc, x, per_channel, gate_w, proj_w, q_w, k_w, v_w, out):
    with ExitStack() as ctx:
        def sb(name, shape, dt=F32):
            return ctx.enter_context(nc.sbuf_tensor(name, shape, dt))

        def sem(name):
            return ctx.enter_context(nc.semaphore(name))

        def flat(t):
            return t.rearrange("p a b -> p (a b)")

        x1_dram = nc.dram_tensor("x1_scratch", (B, C, N), F32, kind="Internal").ap()

        ident = sb("ident", [P, P])
        ident16 = sb("ident16", [P, P], F16)
        zero16 = sb("zero16", [P, P], F16)
        ones = sb("ones", [P, P])
        prm = sb("prm", [P, N_PRM])
        G1, B1, G2, B2, B3, B5, B7, GB, PB, VB, QKB = range(11)
        w3s = prm[:, 11:20]
        w5s = prm[:, 20:45]
        wc = prm[:, 45:94]
        bsum = sb("bsum", [P, 1])
        wT = sb("wT", [P, 5, P])
        WG, WP, WV, WQK = 0, 1, 2, 3
        wstat = sb("wstat", [P, 4])
        wmax = sb("wmax", [P, 4])

        xs = sb("xs", [P, XR, W])
        hp = sb("hp", [P, XR, HW_])
        f = sb("f", [P, NHALF])
        x1 = sb("x1", [P, NHALF])
        bn = sb("bn", [P, NCH, 6])
        mv = sb("mv", [P, 2])
        tot = sb("tot", [P, 2])
        dev = sb("dev", [P, 2])
        var = sb("var", [P, 3])
        aff = sb("aff", [P, 4])
        bnd = sb("bnd", [P, 8])

        Q1 = sb("Q1", [P, N], F16)
        Q2 = sb("Q2", [P, N], F16)
        K1 = sb("K1", [P, N], F16)
        K2 = sb("K2", [P, N], F16)
        vst = sb("vst", [P, 2, 2 * GP, C])
        E = sb("E", [P, NSLOT, 2, CH])
        mxp = sb("mxp", [P, NQT, NBLK])
        m4 = sb("m4", [P, NQT])
        negm = sb("negm", [P, NQT, P], F16)
        accA = sb("accA", [P, 2, CH])
        accB = sb("accB", [P, 2, CH])
        accS = sb("accS", [P, CH])
        pvt = sb("pvt", [P, HCH])
        rec = sb("rec", [P, HCH])
        xst = sb("xst", [P, 2, HCH])
        ot = sb("ot", [P, 2, HCH])

        V = x1[:].rearrange("p (h t c) -> p h t c", h=2, c=C)
        T = E[:, 0:2, :, :].rearrange("p a b c -> p (a b) c")
        gs = E[:, 2, :, :]
        wnat = flat(E[:, 3, :, :])[:, 0:5 * P].rearrange("p (a b) -> p a b", a=5)
        diag = Q1[:, 0:2 * PE_TAPS * P].bitcast(F32).rearrange("p (a b) -> p a b", b=P)

        ps = ctx.enter_context(nc.psum_tensor("ps", [P, 8, CH], F32))
        S_BANK, MX_BANK, ACC_BANK = 0, 4, 6
        STAT_BANK = 3
        x_in = flat(xs[:, PAD:PAD + HR, :])

        prm_in = sem("prm_in")
        mat_in = sem("mat_in")
        x_ready = sem("x_ready")
        const_ready = sem("const_ready")
        pool_step = sem("pool_step")
        dve_step = sem("dve_step")
        wc_ready = sem("wc_ready")
        diag_ready = sem("diag_ready")
        wt_ps = sem("wt_ps")
        wt_ready = sem("wt_ready")
        wmax_ready = sem("wmax_ready")
        wstat_ready = sem("wstat_ready")
        bn_done = sem("bn_done")
        m4_done = sem("m4_done")
        norm_done = sem("norm_done")
        st_in = sem("st_in")
        st_ps = sem("st_ps")
        var_ready = sem("var_ready")
        root_ready = sem("root_ready")
        aff_ready = sem("aff_ready")
        hp_act = sem("hp_act")
        hp_dve = sem("hp_dve")
        cps_ready = sem("cps_ready")
        cps_out = sem("cps_out")
        f_ready = sem("f_ready")
        gate_ready = sem("gate_ready")
        sig_ready = sem("sig_ready")
        fg_ready = sem("fg_ready")
        proj_ready = sem("proj_ready")
        x1_ready = sem("x1_ready")
        x1_stored = sem("x1_stored")
        h_ready = sem("h_ready")
        hmax_ready = sem("hmax_ready")
        hmax_all = sem("hmax_all")
        scale_ready = sem("scale_ready")
        qk_ps = sem("qk_ps")
        t_ready = sem("t_ready")
        hi_ready = sem("hi_ready")
        lo_ready = sem("lo_ready")
        k_moved = sem("k_moved")
        q_first = sem("q_first")
        q_moved = sem("q_moved")
        conv_step = sem("conv_step")
        v_ps = sem("v_ps")
        v_out = sem("v_out")
        mx_ready = sem("mx_ready")
        mx_free = sem("mx_free")
        nm_ready = sem("nm_ready")
        mb_ready = sem("mb_ready")
        m_ready = sem("m_ready")
        s_ready = sem("s_ready")
        e_ready = sem("e_ready")
        pv_free = sem("pv_free")
        adda_free = sem("adda_free")
        addb_free = sem("addb_free")
        vst_ready = [sem("vst_ready0"), sem("vst_ready1")]
        zero_a = sem("zero_a")
        zero_b = sem("zero_b")
        sum_ready = sem("sum_ready")
        rs_ready = sem("rs_ready")
        rs_used = sem("rs_used")
        odd_ready = sem("odd_ready")
        acc_free = sem("acc_free")
        xst_ready = [sem("xst_ready0"), sem("xst_ready1")]
        o_ready = sem("o_ready")
        o_stored = [sem("o_stored0"), sem("o_stored1")]

        MAT_LOADS = [(w, i, h, h) for w, i in ((gate_w, WG), (proj_w, WP), (v_w, WV)) for h in (0, 1)]
        MAT_LOADS += [(w, WQK + h, r, h) for r, w in enumerate((q_w, k_w)) for h in (0, 1)]

        def taps(t):
            dy, dx = divmod(t, 7)
            return dy, dx

        def window(t, r0, rows):
            dy, dx = taps(t)
            return hp[:, r0 + dy:r0 + dy + rows, dx:dx + W]

        def blk(b, j):
            return NBLK * b + j

        def group_of(i):
            return 2 * i[0] + i[1] // GP

        def pair0(b, j):
            return NPAIR * blk(b, j)

        block = ctx.enter_context(nc.Block())

        @block.sync
        def _(sp):
            def load_x(b):
                for h in (0, 1):
                    r = 0 if h == 0 else HR - PAD
                    to = PAD if h == 0 else 0
                    sp.dma_start(xs[C * h:C * h + C, to:to + HR + PAD, :],
                                 x[b, :, r:r + HR + PAD, :]).then_inc(x_ready, 16)

            for par in (0, 1):
                sp.sem_inc(o_stored[par], 32)
            sp.dma_start(prm[:], per_channel[:, :]).then_inc(prm_in, 16)
            load_x(0)
            sp.wait_ge(const_ready, 2)
            for w, i, rh, ch in MAT_LOADS:
                sp.dma_start(wnat[C * rh:C * rh + C, i, C * ch:C * ch + C], w[:, :]).then_inc(mat_in, 16)

            def spread_qk(b):
                third = N // 3
                for n in range(3):
                    cols = slice(n * third, (n + 1) * third)
                    sp.wait_ge(lo_ready, 2 * NCH * b + (n + 1) * third // CH)
                    sp.dma_start(K1[0:C, cols], Q1[C:P, cols]).then_inc(k_moved, 16)
                    sp.dma_start(K2[0:C, cols], Q1[C:P, cols]).then_inc(k_moved, 16)
                    sp.dma_start(K1[C:P, cols], Q2[C:P, cols]).then_inc(k_moved, 16)
                sp.wait_ge(k_moved, 144 * (b + 1))
                sp.dma_start(Q1[C:P, 0:CH], Q1[0:C, 0:CH]).then_inc(q_first, 16)
                sp.dma_start(Q1[C:P, CH:N], Q1[0:C, CH:N]).then_inc(q_moved, 16)

            def load_v(b, j, par, d, gg):
                g = 2 * gg + d
                n = blk(b, j) * NG + g
                slot = (par + d) % 2
                if not (isinstance(n, int) and n < 2):
                    sp.wait_ge(pv_free, GP * n)
                sp.dma_start(flat(vst[:, slot, :, :]), x1[:, bass.ds(g * (2 * GP * C), 2 * GP * C)]
                             ).then_inc(vst_ready[slot], 16)

            def attend(b, j, par, store):
                if b == 0 and isinstance(j, int) and j == 0:
                    for g in range(NG - 1):
                        load_v(b, j, par, g % 2, g // 2)
                else:
                    with sp.Fori(0, NG // 2) as gg:
                        for d in (0, 1):
                            load_v(b, j, par, d, gg)
                load_v(b, j, par, 0, NG // 2)
                if not (b == 0 and isinstance(j, int) and j < 2):
                    sp.wait_ge(o_ready, blk(b, j))
                for h in (0, 1):
                    sp.dma_start(xst[C * h:C * h + C, par, :], x1_dram[b, :, bass.ds(j * CH + h * HCH, HCH)]
                                 ).then_inc(xst_ready[par], 16)
                if store:
                    store_out(b, j - 2, par)

            def store_out(b, j, par):
                sp.wait_ge(o_ready, blk(b, j) + 2)
                for h in (0, 1):
                    sp.dma_start(out[b, :, bass.ds(j * CH + h * HCH, HCH)], ot[C * h:C * h + C, par, :]
                                 ).then_inc(o_stored[par], 16)

            for b in range(B):
                sp.wait_ge(x1_ready, NCH * (b + 1))
                if b + 1 < B:
                    load_x(b + 1)
                for h in (0, 1):
                    sp.dma_start(x1_dram[b, :, h * NHALF:(h + 1) * NHALF], x1[C * h:C * h + C, :]).then_inc(x1_stored, 16)
                spread_qk(b)
                sp.wait_ge(x1_stored, 32 * (b + 1))
                sp.wait_ge(v_out, NCH * (b + 1))
                attend(b, 0, 0, False)
                attend(b, 1, 1, False)
                with sp.Fori(1, NBLK // 2) as jj:
                    for par in (0, 1):
                        attend(b, 2 * jj + par, par, True)
                store_out(b, NBLK - 2, 0)
                store_out(b, NBLK - 1, 1)
            for par in (0, 1):
                sp.wait_ge(o_stored[par], 32 * (B * NBLK // 2 + 1))

        @block.gpsimd
        def _(pool):
            nc.gpsimd.memset(ident[:], 0.0).then_inc(pool_step, 1)
            nc.gpsimd.memset(ones[:], 1.0).then_inc(const_ready, 1)
            nc.gpsimd.memset(flat(wnat), 0.0).then_inc(const_ready, 1)
            pool.wait_ge(pool_step, 1)
            nc.gpsimd.affine_select(out=ident[:], in_=ident[:], compare_op=ALU.not_equal, fill=1.0, base=0,
                                    pattern=[[-1, P]], channel_multiplier=1).then_inc(const_ready, 1)
            nc.gpsimd.memset(zero16[:], 0.0).then_inc(const_ready, 1)
            nc.gpsimd.sem_inc(adda_free, GP + 1)
            pool.wait_ge(wstat_ready, 1)
            nc.gpsimd.partition_all_reduce(wmax[:], wstat[:], P, RMAX).then_inc(wmax_ready, 1)

            def add_a(b, j, par, i):
                n = pair0(b, j) + 2 * GP * i[0] + i[1]
                done = POOL_ADDS * (blk(b, j) * NG + group_of(i)) + GP + 1 + i[1] % GP
                pool.wait_ge(e_ready, n + 2)
                for t in (0, 1) if i[1] % GP == GP - 1 else (0,):
                    pool.wait_ge(adda_free, done + t)
                    nc.gpsimd.tensor_tensor(accA[:, par, :], accA[:, par, :], E[:, i[1] % NSLOT, t, :], ALU.add
                                            ).then_inc(adda_free, 1)

            def total(b, j, par):
                pool.wait_ge(addb_free, DVE_ADDS * (NG * (blk(b, j) + 1) + 1))
                pool.wait_ge(adda_free, POOL_ADDS * (NG * (blk(b, j) + 1) + 1))
                pool.wait_ge(rs_ready, blk(b, j) + 1)
                nc.gpsimd.tensor_tensor(accS[:], accA[:, par, :], accB[:, par, :], ALU.add).then_inc(sum_ready, 1)

            def attend(b, j, par, first=False, last=False):
                with pool.Fori(0, NG // 2) as gg:
                    for p in range(2 * GP):
                        add_a(b, j, par, (gg, p))
                for p in range(GP):
                    if p == 0 and not first:
                        total(b, j - 1, 1 - par)
                    if p == 1 and not first:
                        pool.wait_ge(sum_ready, blk(b, j))
                    add_a(b, j, par, (NG // 2, p))
                    if p == 1 and not last:
                        nc.gpsimd.memset(accA[:, 1 - par, :], 0.0).then_inc(zero_a, 1)
                    if p == 2 and not last:
                        pool.wait_ge(zero_a, blk(b, j) + 2)

            for b in range(B):
                pool.wait_ge(hmax_ready, b + 1)
                nc.gpsimd.partition_all_reduce(bnd[:, 1:2], bnd[:, 0:1], P, RMAX).then_inc(hmax_all, 1)
                if b:
                    pool.wait_ge(sum_ready, blk(b, 0))
                nc.gpsimd.memset(accA[:, 0, :], 0.0).then_inc(zero_a, 1)
                pool.wait_ge(zero_a, blk(b, 0) + 1)
                attend(b, 0, 0, first=True)
                with pool.Fori(0, (NBLK - 2) // 2) as jj:
                    attend(b, 2 * jj + 1, 1)
                    attend(b, 2 * jj + 2, 0)
                attend(b, NBLK - 1, 1, last=True)
                total(b, NBLK - 1, 1)

        @block.scalar
        def _(act):
            act.sem_inc(e_ready, 1)
            def exponentials(b, j, i):
                n = pair0(b, j) + 2 * GP * i[0] + i[1]
                slot, buf, r = i[1] % NSLOT, i[1] % 2, i[1] % GP
                group = NG * blk(b, j) + group_of(i)
                act.wait_ge(s_ready, n + 1)
                act.wait_ge(pv_free, n + 1)
                act.wait_ge(adda_free, POOL_ADDS * group + (1, 2, 3, 5)[r])
                act.wait_ge(addb_free, DVE_ADDS * group + (1, 2, 3, 3)[r])
                nc.scalar.activation(flat(E[:, slot, :, :]), flat(ps[:, S_BANK + 2 * buf:S_BANK + 2 * buf + 2, :]),
                                     ACT.Exp, scale=bnd[:, 6:7]).then_inc(e_ready, 1)

            def move_odd(b, j, par):
                act.wait_ge(pv_free, NSLOT + pair0(b, j) + NPAIR)
                act.wait_ge(o_ready, blk(b, j) + 1)
                for h in (0, 1):
                    nc.scalar.activation(pvt[C * h:C * h + C, :], ps[C:P, ACC_BANK + par, h * HCH:(h + 1) * HCH],
                                         ACT.Copy).then_inc(odd_ready, 1)

            def attend(b, j, par, first=False):
                with act.Fori(0, NG // 2) as gg:
                    for p in range(2 * GP):
                        exponentials(b, j, (gg, p))
                for p in range(GP):
                    exponentials(b, j, (NG // 2, p))
                    if p == 0 and not first:
                        move_odd(b, j - 1, 1 - par)

            def diagonals():
                for t in range(PE_TAPS):
                    a = nc.scalar.activation(diag[:, t, :], ident[:], ACT.Copy,
                                             scale=wc[:, DVE_TAPS + t:DVE_TAPS + t + 1])
                a.then_inc(diag_ready, 1)

            act.wait_ge(const_ready, 3)
            act.wait_ge(wc_ready, 1)
            diagonals()
            def root(n):
                act.wait_ge(var_ready, n + 1)
                nc.scalar.activation(var[:, 1:2], var[:, 0:1], ACT.Sqrt).then_inc(root_ready, 1)

            def pad(b):
                root(2 * b)
                act.wait_ge(aff_ready, 2 * b + 1)
                nc.scalar.activation(hp[0:C, PAD:XR, PAD:PAD + W], xs[0:C, PAD:XR, :], ACT.Identity,
                                     bias=aff[0:C, 1:2], scale=aff[0:C, 0:1]).then_inc(hp_act, 1)

            pad(0)
            for b in range(B):
                for c in range(CCH if b == 0 else 0):
                    act.wait_ge(cps_ready, c + 1)
                    nc.scalar.activation(x1[:, c * CROWS * W:(c + 1) * CROWS * W],
                                         ps[:, c % 4, 0:CROWS * W], ACT.Copy).then_inc(cps_out, 1)
                for c in range(NCH):
                    n = NCH * b + c
                    act.wait_ge(gate_ready, n + 1)
                    if c >= 2:
                        act.wait_ge(fg_ready, n - 1)
                    nc.scalar.activation(gs[:, c % 2, :], ps[:, c % 2, :], ACT.Sigmoid,
                                         bias=prm[:, GB:GB + 1]).then_inc(sig_ready, 1)
                root(2 * b + 1)
                act.wait_ge(aff_ready, 2 * b + 2)
                nc.scalar.activation(f[:], x1[:], ACT.Identity, bias=aff[:, 3:4], scale=aff[:, 2:3]).then_inc(h_ready, 1)
                act.wait_ge(scale_ready, b + 1)
                for c in range(2 * NCH):
                    n = 2 * NCH * b + c
                    act.wait_ge(qk_ps, n + 1)
                    if n >= 4:
                        act.wait_ge(lo_ready, n - 3)
                    nc.scalar.activation(T[:, c % 4, :], ps[:, c % 3, :], ACT.Identity,
                                         bias=bnd[:, 5:6], scale=bnd[:, 4:5]).then_inc(t_ready, 1)
                    nc.scalar.activation(Q1[:, c * CH:(c + 1) * CH], ps[:, c % 3, :], ACT.Identity,
                                         bias=bnd[:, 5:6], scale=bnd[:, 4:5]).then_inc(hi_ready, 1)
                if b + 1 < B:
                    pad(b + 1)
                    act.wait_ge(v_ps, NCH * (b + 1))
                    nc.scalar.activation(f[:], bsum[:].to_broadcast([P, NHALF]), ACT.Copy).then_inc(conv_step, 1)
                attend(b, 0, 0, first=True)
                with act.Fori(0, (NBLK - 2) // 2) as jj:
                    attend(b, 2 * jj + 1, 1)
                    attend(b, 2 * jj + 2, 0)
                attend(b, NBLK - 1, 1)
                move_odd(b, NBLK - 1, 1)

        @block.vector
        def _(dve):
            steps = [0]

            def chain(ins):
                steps[0] += 1
                ins.then_inc(dve_step, 1)
                dve.wait_ge(dve_step, steps[0])

            nc.vector.memset(hp[:].rearrange("p a b -> p (a b)"), 0.0).then_inc(dve_step, 1)
            steps[0] += 1
            dve.sem_inc(acc_free, 4)
            dve.sem_inc(rs_used, 1)
            dve.sem_inc(o_ready, 1)
            dve.sem_inc(mx_free, 2)
            dve.sem_inc(addb_free, DVE_ADDS)
            dve.wait_ge(const_ready, 3)
            nc.vector.tensor_copy(ident16[:], ident[:]).then_inc(const_ready, 1)
            nc.vector.memset(K2[C:P, :], ONE).then_inc(const_ready, 1)
            dve.wait_ge(prm_in, 16)
            for k, src in ((5, w5s), (3, w3s)):
                o = (7 - k) // 2
                mid = wc.rearrange("p (y x) -> p y x", x=7)[:, o:o + k, o:o + k]
                chain(nc.vector.tensor_tensor(mid, mid, src.rearrange("p (y x) -> p y x", x=k), ALU.add))
            chain(nc.vector.tensor_tensor(bsum[:], prm[:, B3:B3 + 1], prm[:, B5:B5 + 1], ALU.add))
            nc.vector.tensor_tensor(bsum[:], bsum[:], prm[:, B7:B7 + 1], ALU.add).then_inc(wc_ready, 1)

            def weight_norms():
                dve.wait_ge(wt_ps, 1)
                nc.vector.tensor_copy(flat(wT[:, 0:4, :]), ps[:, 4, :])
                nc.vector.tensor_copy(wT[:, 4, :], ps[:, 5, 0:P]).then_inc(wt_ready, 1)
                chain(nc.vector.memset(wstat[:], 0.0))
                for k in (0, 1):
                    rows = slice(C * k, C * k + C)
                    nc.vector.tensor_reduce(wstat[rows, k:k + 1], wnat[rows, WQK, :], AX.X, ALU.add,
                                            apply_absolute_value=True)
                    last = nc.vector.tensor_reduce(wstat[rows, 2 + k:3 + k], prm[rows, QKB:QKB + 1], AX.X, ALU.max,
                                                   apply_absolute_value=True)
                last.then_inc(wstat_ready, 1)

            def norm(b, second, gamma, beta, col):
                dve.wait_ge(bn_done, NCH * (2 * b + second + 1))
                nc.vector.bn_aggr(mv[:], bn[:].rearrange("p a b -> p (a b)")).then_inc(st_in, 1)
                dve.wait_ge(st_ps, 4 * b + 2 * second + 1)
                chain(nc.vector.tensor_scalar(tot[:], ps[:, STAT_BANK, 0:2], 1.0 / P, None, ALU.mult))
                chain(nc.vector.tensor_tensor(dev[:, 0:1], mv[:, 0:1], tot[:, 0:1], ALU.subtract))
                nc.vector.tensor_tensor(dev[:, 1:2], dev[:, 0:1], dev[:, 0:1], ALU.mult).then_inc(st_in, 1)
                dve.wait_ge(st_ps, 4 * b + 2 * second + 2)
                chain(nc.vector.scalar_tensor_tensor(out=tot[:, 1:2], in0=ps[:, STAT_BANK, 2:3], scalar=1.0 / P,
                                                     in1=tot[:, 1:2], op0=ALU.mult, op1=ALU.add))
                nc.vector.tensor_scalar(var[:, 0:1], tot[:, 1:2], EPS, None, ALU.add).then_inc(var_ready, 1)
                dve.wait_ge(root_ready, 2 * b + second + 1)
                chain(nc.vector.reciprocal(tot[:, 1:2], var[:, 1:2]))
                chain(nc.vector.tensor_tensor(var[:, 2:3], tot[:, 1:2], tot[:, 1:2], ALU.mult))
                chain(nc.vector.tensor_tensor(var[:, 2:3], var[:, 2:3], var[:, 0:1], ALU.mult))
                chain(nc.vector.tensor_scalar(var[:, 2:3], var[:, 2:3], -0.5, 1.5, ALU.mult, ALU.add))
                chain(nc.vector.tensor_tensor(tot[:, 1:2], tot[:, 1:2], var[:, 2:3], ALU.mult))
                chain(nc.vector.tensor_tensor(aff[:, col:col + 1], prm[:, gamma:gamma + 1], tot[:, 1:2], ALU.mult))
                chain(nc.vector.tensor_tensor(tot[:, 0:1], tot[:, 0:1], aff[:, col:col + 1], ALU.mult))
                nc.vector.tensor_tensor(aff[:, col + 1:col + 2], prm[:, beta:beta + 1], tot[:, 0:1],
                                        ALU.subtract).then_inc(aff_ready, 1)

            def reduce_max(m, at, c):
                dve.wait_ge(mx_ready, m + 1)
                nc.vector.reduce_max(at, ps[:, MX_BANK + c % 2, :], AX.X).then_inc(mx_free, 1)

            def maxima(b, j):
                f0 = blk(b, j)
                dve.wait_ge(mx_free, 2 + NMX * (f0 + 1))
                nc.vector.reduce_max(m4[:], mxp[:], AX.X).then_inc(m4_done, 1)
                dve.wait_ge(m4_done, f0 + 1)
                dve.wait_ge(mb_ready, f0)
                nc.vector.tensor_scalar(negm[:], m4[:].unsqueeze(2).to_broadcast([P, NQT, P]), -M_ROW, None,
                                        ALU.mult).then_inc(nm_ready, 1)

            def place_maxima(b, j):
                dve.wait_ge(mb_ready, blk(b, j) + 1)
                nc.vector.tensor_copy(Q2[C:P, bass.ds(j * CH, CH)], ps[C:P, MX_BANK, :]).then_inc(m_ready, 1)

            def add_b(b, j, par, i):
                n = pair0(b, j) + 2 * GP * i[0] + i[1]
                dve.wait_ge(e_ready, n + 2)
                dve.wait_ge(addb_free, DVE_ADDS * (NG * blk(b, j) + group_of(i) + 1) + i[1] % GP)
                nc.vector.tensor_tensor(accB[:, par, :], accB[:, par, :], E[:, i[1] % NSLOT, 1, :], ALU.add
                                        ).then_inc(addb_free, 1)

            def conv_tap(dy, dx, strip, done):
                dve.wait_ge(conv_step, 1 + done)
                at = f[:, bass.ds(strip * (SROWS * W), SROWS * W)].rearrange("p (y x) -> p y x", x=W)
                src = flat(hp[:])[:, bass.ds((strip * SROWS + dy) * HW_, SROWS * HW_)]
                nc.vector.scalar_tensor_tensor(out=at, in0=src.rearrange("p (y x) -> p y x", x=HW_)[:, :, dx:dx + W],
                                               scalar=wc[:, bass.ds(7 * dy + dx, 1)], in1=at,
                                               op0=ALU.mult, op1=ALU.add).then_inc(conv_step, 1)

            def attend(b, j, par, first=False, last=False, jhalf=None, taps=(), done=0):
                m0 = NMX * (blk(b, j) + 1)
                with dve.Fori(0, NG // 2) as gg:
                    c = 0
                    for p in range(2 * GP):
                        for _ in range(0 if last else 2):
                            reduce_max(m0 + NBLK * gg + c, mxp_at(gg, c), c)
                            c += 1
                        if p % GP < DVE_ADDS:
                            add_b(b, j, par, (gg, p))
                        if p % GP == GP - 1 and not last:
                            reduce_max(m0 + NBLK * gg + c, mxp_at(gg, c), c)
                            c += 1
                        for k, (dy, dx, strip) in enumerate(taps):
                            if k * 2 * GP // len(taps) == p:
                                conv_tap(dy, dx, strip + gg, done + len(taps) * gg + k)
                if not last:
                    maxima(b, j + 1)
                for p in range(GP):
                    if p == 1 and not last:
                        place_maxima(b, j + 1)
                    if p == 2 and not last:
                        dve.wait_ge(zero_b, blk(b, j) + 2)
                    if p < DVE_ADDS:
                        add_b(b, j, par, (NG // 2, p))
                    if p == 1 and not first:
                        finish(b, j - 1, 1 - par, jhalf)
                    if p == 1 and not last:
                        dve.wait_ge(sum_ready, blk(b, j))
                        nc.vector.memset(accB[:, 1 - par, :], 0.0).then_inc(zero_b, 1)

            def attend_and_convolve(b):
                half = STRIPS // 2
                both = lambda dys, dx: [(dy, dx, s) for dy in dys for s in (0, half)]
                loop = [[(0, dx, s) for dx in range(5)] for s in (0, half)]
                head = both((0, 1), 5)
                tail = [both((2, 3), 5) + [(4, 5, 0)], both((5, 6), 5) + [(4, 5, half)], both(range(7), 6)]
                done = 0
                attend(b, 0, 0, first=True, taps=head, done=done)
                done += half * len(head)
                each = half * len(loop[0])
                with dve.Fori(0, 7) as jj:
                    for par in (1, 0):
                        taps = [(jj, dx, s) for _, dx, s in loop[1 - par]]
                        attend(b, 2 * jj + 2 - par, par, jhalf=jj, taps=taps,
                               done=done + each * (2 * jj + 1 - par))
                done += 7 * 2 * each
                for j, taps in zip(range(NBLK - 3, NBLK), tail):
                    attend(b, j, j % 2, last=(j == NBLK - 1), taps=taps, done=done)
                    done += half * len(taps)
                assert done == TAPS * STRIPS

            def mxp_at(gg, c):
                return flat(mxp[:])[:, bass.ds(NBLK * gg + c, 1)]

            def finish(b, j, par, jhalf):
                f0 = blk(b, j)
                done = (b * (NBLK // 2) + (j // 2 if jhalf is None else jhalf)) * 32
                dve.wait_ge(odd_ready, 2 * f0 + 2)
                for h in (0, 1):
                    rows = slice(C * h, C * h + C)
                    nc.vector.tensor_tensor(pvt[rows, :], ps[0:C, ACC_BANK + par, h * HCH:(h + 1) * HCH], pvt[rows, :],
                                            ALU.add).then_inc(acc_free, 1)
                dve.wait_ge(rs_ready, f0 + 2)
                nc.vector.reciprocal(rec[:], ps[:, MX_BANK + 1, 0:HCH]).then_inc(rs_used, 1)
                dve.wait_ge(acc_free, 2 * f0 + 6)
                dve.wait_ge(rs_used, f0 + 2)
                nc.vector.tensor_tensor(pvt[:], pvt[:], rec[:], ALU.mult).then_inc(norm_done, 1)
                dve.wait_ge(norm_done, f0 + 1)
                dve.wait_ge(xst_ready[par], done + 32)
                dve.wait_ge(o_stored[par], done + 32)
                nc.vector.scalar_tensor_tensor(out=ot[:, par, :], in0=pvt[:], scalar=prm[:, VB:VB + 1],
                                               in1=xst[:, par, :], op0=ALU.add, op1=ALU.add).then_inc(o_ready, 1)

            def x_stats(b, c):
                nc.vector.bn_stats(bn[:, c, :], x_in[:, c * CH:(c + 1) * CH]).then_inc(bn_done, 1)

            def pad(b):
                norm(b, 0, G1, B1, 0)
                dve.wait_ge(aff_ready, 2 * b + 1)
                nc.vector.tensor_scalar(hp[C:P, 0:HR + PAD, PAD:PAD + W], xs[C:P, 0:HR + PAD, :], aff[C:P, 0:1],
                                        aff[C:P, 1:2], ALU.mult, ALU.add).then_inc(hp_dve, 1)
                dve.wait_ge(hp_act, b + 1)
                dve.wait_ge(hp_dve, b + 1)

            dve.wait_ge(x_ready, 32)
            for c in range(NCH):
                x_stats(0, c)
            pad(0)
            for b in range(B):
                if b == 0:
                    f3 = f[:].rearrange("p (y x) -> p y x", x=W)
                    chain(nc.vector.tensor_scalar(f3, window(0, 0, HR), wc[:, 0:1], bsum[:], ALU.mult, ALU.add))
                    for t in range(1, DVE_TAPS):
                        chain(nc.vector.scalar_tensor_tensor(out=f3, in0=window(t, 0, HR), scalar=wc[:, t:t + 1],
                                                             in1=f3, op0=ALU.mult, op1=ALU.add))
                    weight_norms()
                    dve.wait_ge(cps_out, CCH)
                    nc.vector.tensor_tensor(f[:], f[:], x1[:], ALU.add).then_inc(f_ready, 1)
                    dve.wait_ge(f_ready, 1)
                else:
                    dve.wait_ge(conv_step, 1 + TAPS * STRIPS)

                def gated(c):
                    dve.wait_ge(sig_ready, NCH * b + c + 1)
                    at = f[:, c * CH:(c + 1) * CH]
                    nc.vector.tensor_tensor(at, at, gs[:, c % 2, :], ALU.mult).then_inc(fg_ready, 1)

                gated(0)
                for c in range(NCH):
                    n = NCH * b + c
                    if c + 1 < NCH:
                        gated(c + 1)
                    dve.wait_ge(proj_ready, n + 1)
                    at = x1[:, c * CH:(c + 1) * CH]
                    nc.vector.scalar_tensor_tensor(out=at, in0=ps[:, 2 + c % 2, :], scalar=prm[:, PB:PB + 1],
                                                   in1=x_in[:, c * CH:(c + 1) * CH], op0=ALU.add,
                                                   op1=ALU.add).then_inc(x1_ready, 1)
                    dve.wait_ge(x1_ready, n + 1)
                    nc.vector.bn_stats(bn[:, c, :], at).then_inc(bn_done, 1)
                norm(b, 1, G2, B2, 2)
                dve.wait_ge(h_ready, b + 1)
                nc.vector.tensor_reduce(bnd[:, 0:1], f[:], AX.X, ALU.max, apply_absolute_value=True).then_inc(hmax_ready, 1)
                dve.wait_ge(hmax_all, b + 1)
                dve.wait_ge(wmax_ready, 1)
                chain(nc.vector.scalar_tensor_tensor(out=bnd[:, 2:4], in0=wmax[:, 0:2], scalar=bnd[:, 1:2],
                                                     in1=wmax[:, 2:4], op0=ALU.mult, op1=ALU.add))
                chain(nc.vector.tensor_scalar(bnd[:, 2:4], bnd[:, 2:4], 1e-12, 1.0 / QK_TOP, ALU.max, ALU.mult))
                for k in (0, 1):
                    rows = slice(C * k, C * k + C)
                    chain(nc.vector.reciprocal(bnd[rows, 4:5], bnd[rows, 2 + k:3 + k]))
                chain(nc.vector.tensor_tensor(bnd[:, 5:6], bnd[:, 4:5], prm[:, QKB:QKB + 1], ALU.mult))
                chain(nc.vector.tensor_tensor(bnd[:, 6:7], bnd[:, 2:3], bnd[:, 3:4], ALU.mult))
                nc.vector.tensor_scalar(bnd[:, 6:7], bnd[:, 6:7], C ** -0.5, None, ALU.mult).then_inc(scale_ready, 1)
                for c in range(2 * NCH):
                    n = 2 * NCH * b + c
                    cols = slice(c * CH, (c + 1) * CH)
                    dve.wait_ge(t_ready, n + 1)
                    dve.wait_ge(hi_ready, n + 1)
                    nc.vector.tensor_tensor(Q2[:, cols], T[:, c % 4, :], Q1[:, cols], ALU.subtract).then_inc(lo_ready, 1)
                    if b + 1 < B and c >= NCH:
                        dve.wait_ge(x_ready, 32 * (b + 2))
                        x_stats(b + 1, c - NCH)
                if b + 1 < B:
                    pad(b + 1)
                dve.wait_ge(x1_stored, 32 * (b + 1))
                for g in range(NCH):
                    for q in range(8):
                        c = 8 * g + q
                        reduce_max(NMX * blk(b, 0) + c, flat(mxp[:])[:, c:c + 1], c)
                    dve.wait_ge(v_ps, NCH * b + g + 1)
                    nc.vector.tensor_copy(V[:, :, NQT * g:NQT * g + NQT, :].rearrange("p h t c -> p t h c"),
                                          ps[:, ACC_BANK + g % 2, :].rearrange("p (t h c) -> p t h c", t=NQT, h=2)
                                          ).then_inc(v_out, 1)
                maxima(b, 0)
                dve.wait_ge(k_moved, 144 * (b + 1))
                place_maxima(b, 0)
                if b:
                    dve.wait_ge(sum_ready, blk(b, 0))
                nc.vector.memset(accB[:, 0, :], 0.0).then_inc(zero_b, 1)
                dve.wait_ge(zero_b, blk(b, 0) + 1)
                if b + 1 == B:
                    attend(b, 0, 0, first=True)
                    with dve.Fori(0, (NBLK - 2) // 2) as jj:
                        attend(b, 2 * jj + 1, 1, jhalf=jj)
                        attend(b, 2 * jj + 2, 0, jhalf=jj)
                    attend(b, NBLK - 1, 1, last=True)
                else:
                    attend_and_convolve(b)
                finish(b, NBLK - 1, 1, None)

        @block.tensor
        def _(pe):
            pe.sem_inc(rs_ready, 1)
            pe.sem_inc(pv_free, NSLOT)
            pe.wait_ge(const_ready, 6)

            def transpose_weights():
                pe.wait_ge(mat_in, 16 * len(MAT_LOADS))
                for i in range(5):
                    a = nc.tensor.transpose(ps[:, 4 + i // 4, (i % 4) * P:(i % 4 + 1) * P], wnat[:, i, :], ident[:])
                a.then_inc(wt_ps, 1)

            def stats(n):
                pe.wait_ge(st_in, n + 1)
                nc.tensor.matmul(ps[:, STAT_BANK, 0:2], ones[:], mv[:], start=True, stop=True).then_inc(st_ps, 1)
                pe.wait_ge(st_in, n + 2)
                nc.tensor.matmul(ps[:, STAT_BANK, 2:3], ones[:], dev[:, 1:2], start=True, stop=True).then_inc(st_ps, 1)

            def scores(b, j, i, n, peers):
                base, p = i
                buf = p % 2
                if peers is not None:
                    pe.wait_ge(e_ready, peers + 1)
                for t in (0, 1):
                    k = bass.ds((2 * GP * base + p) * 2 * P + t * P, P)
                    dst = ps[:, S_BANK + 2 * buf + t, :]
                    nc.tensor.matmul(dst, K1[:, k], Q1[:, bass.ds(j * CH, CH)], start=True, stop=False)
                    a = nc.tensor.matmul(dst, K2[:, k], Q2[:, bass.ds(j * CH, CH)], start=False, stop=True)
                a.then_inc(s_ready, 1)

            def weigh(b, par, p, n, slot):
                pe.wait_ge(e_ready, n + 2)
                for t in (0, 1):
                    a = nc.tensor.matmul(ps[C * t:C * t + C, ACC_BANK + par, :], vst[:, slot, 2 * (p % GP) + t, :],
                                         E[:, p % NSLOT, t, :], start=False, stop=False, skip_group_check=True)
                a.then_inc(pv_free, 1)

            def max_scores(j, qt, m, c):
                pe.wait_ge(mx_free, m + 1)
                nc.tensor.matmul(ps[:, MX_BANK + c % 2, :], Q1[:, bass.ds(j * CH + qt * P, P)],
                                 K1[:, (c % NBLK) * CH:(c % NBLK + 1) * CH], start=True, stop=True).then_inc(mx_ready, 1)

            def spread_maxima(b, j):
                pe.wait_ge(nm_ready, blk(b, j) + 1)
                for q in range(NQT):
                    a = nc.tensor.matmul(ps[:, MX_BANK, q * P:(q + 1) * P], negm[:, q, :], ident16[:], start=True, stop=True)
                a.then_inc(mb_ready, 1)

            def row_sums(b, j):
                pe.wait_ge(sum_ready, blk(b, j) + 1)
                for h in (0, 1):
                    a = nc.tensor.matmul(ps[C * h:C * h + C, MX_BANK + 1, 0:HCH], ones[:, 0:C],
                                         accS[:, h * HCH:(h + 1) * HCH], start=True, stop=True)
                a.then_inc(rs_ready, 1)

            def vst_wait(b, j, par, jhalf, d, gg):
                slot = (par + d) % 2
                n = NG * (blk(b, 0) // 2) + NG * jhalf + (NG * par + d) // 2 + gg
                pe.wait_ge(vst_ready[slot], 16 * (n + 1))
                return slot

            def attend(b, j, par, jhalf, first=False, last=False):
                n0 = pair0(b, j)
                m0 = NMX * (blk(b, j) + 1)
                pe.wait_ge(acc_free, 2 * blk(b, j) + 2)
                if not first:
                    pe.wait_ge(rs_used, blk(b, j))
                nc.tensor.matmul(ps[:, ACC_BANK + par, :], zero16[:], Q1[:, 0:CH], start=True, stop=True)
                with pe.Fori(0, NG // 2) as gg:
                    c = 0
                    for p in range(2 * GP):
                        n = n0 + 2 * GP * gg + p
                        scores(b, j, (gg, p + 1), n + 1, n)
                        for _ in range(0 if last else 2):
                            max_scores(j + 1, gg, m0 + NBLK * gg + c, c)
                            c += 1
                        if p % GP == 0:
                            slot = vst_wait(b, j, par, jhalf, p // GP, gg)
                        weigh(b, par, p, n, slot)
                        if p % GP == GP - 1 and not last:
                            max_scores(j + 1, gg, m0 + NBLK * gg + c, c)
                            c += 1
                slot = vst_wait(b, j, par, jhalf, NG - 1, 0)
                for p in range(GP):
                    n = n0 + NPAIR - GP + p
                    if p < GP - 1:
                        scores(b, j, (NG // 2, p + 1), n + 1, n)
                    elif not last:
                        pe.wait_ge(m_ready, blk(b, j) + 2)
                        scores(b, j + 1, (0, 0), n + 1, n)
                    if p == 1 and not last:
                        spread_maxima(b, j + 1)
                    if p == 2 and not first:
                        row_sums(b, j - 1)
                    weigh(b, par, p, n, slot)

            stats(0)
            pe.wait_ge(diag_ready, 1)
            pe.wait_ge(hp_act, 1)
            pe.wait_ge(hp_dve, 1)
            for c in range(CCH):
                if c >= 4:
                    pe.wait_ge(cps_out, c - 3)
                for t in range(PE_TAPS):
                    a = nc.tensor.matmul(ps[:, c % 4, 0:CROWS * W].rearrange("p (y x) -> p y x", x=W),
                                         diag[:, t, :], window(DVE_TAPS + t, c * CROWS, CROWS),
                                         start=(t == 0), stop=(t == PE_TAPS - 1))
                a.then_inc(cps_ready, 1)
            transpose_weights()
            pe.wait_ge(wt_ready, 1)

            for b in range(B):
                if b:
                    pe.wait_ge(o_ready, NBLK * b + 1)

                def gate(c):
                    n = NCH * b + c
                    if c >= 2:
                        pe.wait_ge(sig_ready, n - 1)
                    nc.tensor.matmul(ps[:, c % 2, :], wT[:, WG, :], f[:, c * CH:(c + 1) * CH], start=True,
                                     stop=True).then_inc(gate_ready, 1)

                if b:
                    pe.wait_ge(conv_step, 1 + TAPS * STRIPS)
                else:
                    pe.wait_ge(f_ready, 1)
                gate(0)
                for c in range(NCH):
                    n = NCH * b + c
                    if c + 1 < NCH:
                        gate(c + 1)
                    pe.wait_ge(fg_ready, n + 1)
                    if c >= 2:
                        pe.wait_ge(x1_ready, n - 1)
                    nc.tensor.matmul(ps[:, 2 + c % 2, :], wT[:, WP, :], f[:, c * CH:(c + 1) * CH], start=True,
                                     stop=True).then_inc(proj_ready, 1)
                stats(4 * b + 2)
                pe.wait_ge(h_ready, b + 1)
                for c in range(2 * NCH):
                    h, cc = divmod(c, NCH)
                    n = 2 * NCH * b + c
                    if c >= 3:
                        pe.wait_ge(hi_ready, n - 2)
                    nc.tensor.matmul(ps[:, c % 3, :], wT[:, WQK + h, :], f[:, cc * CH:(cc + 1) * CH], start=True,
                                     stop=True).then_inc(qk_ps, 1)
                if b + 1 < B:
                    stats(4 * (b + 1))
                pe.wait_ge(k_moved, 144 * (b + 1))
                pe.wait_ge(q_first, 16 * (b + 1))
                for g in range(NCH):
                    if g >= 2:
                        pe.wait_ge(v_out, NCH * b + g - 1)
                    for q in range(8):
                        c = 8 * g + q
                        max_scores(0, c // NBLK, NMX * blk(b, 0) + c, c)
                        if q % 2:
                            t = NQT * g + q // 2
                            a = nc.tensor.matmul(ps[:, ACC_BANK + g % 2, (q // 2) * P:(q // 2 + 1) * P],
                                                 f[:, t * P:(t + 1) * P], wT[:, WV, :], start=True, stop=True)
                    a.then_inc(v_ps, 1)
                spread_maxima(b, 0)
                pe.wait_ge(q_moved, 16 * (b + 1))
                if b + 1 < B:
                    pe.wait_ge(aff_ready, 2 * b + 3)
                pe.wait_ge(v_out, NCH * (b + 1))
                pe.wait_ge(m_ready, blk(b, 0) + 1)
                scores(b, 0, (0, 0), pair0(b, 0), None)
                attend(b, 0, 0, 0, first=True)
                with pe.Fori(0, (NBLK - 2) // 2) as jj:
                    attend(b, 2 * jj + 1, 1, jj)
                    attend(b, 2 * jj + 2, 0, jj + 1)
                attend(b, NBLK - 1, 1, NBLK // 2 - 1, last=True)
                row_sums(b, NBLK - 1)


def kernel(**inputs):
    import concourse.bacc as bacc
    from concourse.bass_utils import run_bass_kernel_spmd

    nc = bacc.Bacc("TRN2", target_bir_lowering=False, num_devices=1)
    raw = {n.removeprefix("L0_conv_"): np.asarray(a) for n, a in inputs.items()}
    both = ("n1_g", "n1_b", "n2_g", "n2_b", "b3", "b5", "b7", "gate_b", "proj_b", "v_b")
    columns = [np.tile(raw[n], 2)[:, None] for n in both]
    columns += [np.concatenate([raw["q_b"], raw["k_b"]])[:, None]]
    columns += [np.tile(raw[n].reshape(C, -1), (2, 1)) for n in ("w3", "w5", "w7")]
    given = {"x": raw["x"], "per_channel": np.concatenate(columns, axis=1)}
    given.update({n: raw[n] for n in ("gate_w", "proj_w", "q_w", "k_w", "v_w")})
    arrays, args = {}, []
    for name, a in given.items():
        arrays[f"in_{name}"] = a = np.ascontiguousarray(a)
        args.append(nc.dram_tensor(f"in_{name}", a.shape, mybir.dt.from_np(a.dtype), kind="ExternalInput").ap())
    out = nc.dram_tensor("out", (B, C, N), F32, kind="ExternalOutput").ap()
    program(nc, *args, out)
    r = run_bass_kernel_spmd(nc, [arrays], core_ids=[0])
    return r.results[0]["out"].reshape(B, C, H, W)
```

```python
from contextlib import ExitStack

import numpy as np

import concourse.bass as bass
from concourse import mybir

F32 = mybir.dt.float32
F16 = mybir.dt.float16
ALU = mybir.AluOpType
ACT = mybir.ActivationFunctionType
AX = mybir.AxisListType
RMAX = bass.bass_isa.ReduceOp.max

B, C, H, W = 2, 64, 96, 96
P = 128
N = H * W
HR = H // 2
NHALF = HR * W
PAD = 3
XR = HR + 2 * PAD
HW_ = W + 2 * PAD
EPS = 1e-5

CH = 512
HCH = CH // 2
NCH = NHALF // CH
NBLK = N // CH
NPAIR = N // (2 * P)
NQT = CH // P
NMX = NQT * NBLK
GP = 4
NG = NPAIR // GP
STRIPS = 8
SROWS = HR // STRIPS
NSLOT = GP
PIECE = 2
NPIECE = 2 * NCH // PIECE
MX_FROM = 5
MX_BESIDE = 2 * (2 * NCH - MX_FROM)
H_ACT = 4
POOL_ODD = (1, 3)
POOL_DONE = [r + sum(q < r for q in POOL_ODD) for r in range(GP + 1)]
DVE_DONE = [r - sum(q < r for q in POOL_ODD) for r in range(GP + 1)]
POOL_ADDS, DVE_ADDS = POOL_DONE[GP], DVE_DONE[GP]

TAPS = 49
TAP_AT = {4: (0, 1, 4, 5), 5: (0, 1, 3, 5, 7), 14: (0, 0, 1, 1, 2, 2, 3, 3, 4, 4, 5, 5, 6, 7)}
N_PRM = 11 + 9 + 25 + TAPS
DVE_TAPS = 22
POOL_TAPS = 12
PE_TAPS = TAPS - DVE_TAPS - POOL_TAPS
FIRST_ADD = 5
CROWS = 4
BAND = -(-HR * 5 // 9)
CCH = HR // CROWS
QK_TOP = 2.0 ** 14
ONE = 2.0 ** 14
M_ROW = 1.0 / (ONE * 64)


def program(nc, x, per_channel, gate_w, proj_w, q_w, k_w, v_w, out):
    with ExitStack() as ctx:
        def sb(name, shape, dt=F32):
            return ctx.enter_context(nc.sbuf_tensor(name, shape, dt))

        def sem(name):
            return ctx.enter_context(nc.semaphore(name))

        def flat(t):
            return t.rearrange("p a b -> p (a b)")

        x1_dram = nc.dram_tensor("x1_scratch", (B, C, N), F32, kind="Internal").ap()

        ident = sb("ident", [P, P])
        ident16 = sb("ident16", [P, P], F16)
        zero16 = sb("zero16", [P, P], F16)
        ones = sb("ones", [P, P])
        prm = sb("prm", [P, N_PRM])
        G1, B1, G2, B2, B3, B5, B7, GB, PB, VB, QKB = range(11)
        w3s = prm[:, 11:20]
        w5s = prm[:, 20:45]
        wc = prm[:, 45:94]
        bsum = sb("bsum", [P, 1])
        wT = sb("wT", [P, 5, P])
        WG, WP, WV, WQK = 0, 1, 2, 3
        wstat = sb("wstat", [P, 4])
        wmax = sb("wmax", [P, 4])

        xs = sb("xs", [P, XR, W])
        hp = sb("hp", [P, XR, HW_])
        f = sb("f", [P, NHALF])
        x1 = sb("x1", [P, NHALF])
        bn = sb("bn", [P, NCH, 6])
        mv = sb("mv", [P, 2])
        tot = sb("tot", [P, 2])
        dev = sb("dev", [P, 2])
        var = sb("var", [P, 3])
        aff = sb("aff", [P, 4])
        x1_max = sb("x1_max", [P, NCH])
        aff_abs = sb("aff_abs", [P, 2])
        bnd = sb("bnd", [P, 8])

        Q0 = sb("Q0", [P, CH], F16)
        Q1 = sb("Q1", [P, N], F16)
        Q2 = sb("Q2", [P, N], F16)
        K1 = sb("K1", [P, N], F16)
        K2 = sb("K2", [P, N], F16)
        vst = sb("vst", [P, 2, 2 * GP, C])
        E = sb("E", [P, NSLOT, 2, CH])
        mxp = sb("mxp", [P, NQT, NBLK])
        m4 = sb("m4", [P, NQT])
        negm = sb("negm", [P, NQT, P], F16)
        accA = sb("accA", [P, 2, CH])
        accB = sb("accB", [P, 2, CH])
        accS = sb("accS", [P, CH])
        pvt = sb("pvt", [P, HCH])
        rec = sb("rec", [P, HCH])
        xst = sb("xst", [P, 2, HCH])
        ot = sb("ot", [P, 2, HCH])

        V = x1[:].rearrange("p (h t c) -> p h t c", h=2, c=C)
        T = E[:, 0:2, :, :].rearrange("p a b c -> p (a b) c")
        gs = E[:, 2:4, :, :].rearrange("p a b c -> p (a b) c")
        prod = Q2[:].bitcast(F32).rearrange("p (h n) -> p h n", h=2)
        wnat = flat(E[:, 3, :, :])[:, 0:5 * P].rearrange("p (a b) -> p a b", a=5)
        diag = Q1[:, 0:2 * PE_TAPS * P].bitcast(F32).rearrange("p (a b) -> p a b", b=P)

        ps = ctx.enter_context(nc.psum_tensor("ps", [P, 8, CH], F32))
        S_BANK, MX_BANK, ACC_BANK = 0, 4, 6
        STAT_BANK = 3
        PROJ_BANK = 3
        x_in = flat(xs[:, PAD:PAD + HR, :])

        prm_in = sem("prm_in")
        mat_in = sem("mat_in")
        x_ready = [sem("x_ready0"), sem("x_ready1")]
        const_ready = sem("const_ready")
        pool_step = sem("pool_step")
        dve_step = sem("dve_step")
        wc_ready = sem("wc_ready")
        diag_ready = sem("diag_ready")
        wt_ps = sem("wt_ps")
        wt_ready = sem("wt_ready")
        wmax_ready = sem("wmax_ready")
        wstat_ready = sem("wstat_ready")
        bn_done = sem("bn_done")
        m4_done = sem("m4_done")
        norm_done = sem("norm_done")
        st_in = sem("st_in")
        st_ps = sem("st_ps")
        var_ready = sem("var_ready")
        root_ready = sem("root_ready")
        aff_ready = sem("aff_ready")
        hp_zero = sem("hp_zero")
        hp_act = sem("hp_act")
        hp_dve = sem("hp_dve")
        cps_ready = sem("cps_ready")
        cps_out = sem("cps_out")
        prod_ready = sem("prod_ready")
        prod_added = sem("prod_added")
        f_ready = sem("f_ready")
        gate_ready = sem("gate_ready")
        sig_ready = sem("sig_ready")
        fg_ready = sem("fg_ready")
        proj_ready = sem("proj_ready")
        x1_ready = sem("x1_ready")
        x1_stored = sem("x1_stored")
        x1_maxed = sem("x1_maxed")
        h_act = sem("h_act")
        h_dve = sem("h_dve")
        hmax_ready = sem("hmax_ready")
        hmax_all = sem("hmax_all")
        scale_ready = sem("scale_ready")
        qk_ps = sem("qk_ps")
        t_ready = sem("t_ready")
        hi_ready = sem("hi_ready")
        lo_ready = sem("lo_ready")
        k_moved = [sem(f"k_moved{n}") for n in range(NPIECE)]
        k2_moved = sem("k2_moved")
        q_first = sem("q_first")
        q_moved = sem("q_moved")
        conv_step = sem("conv_step")
        v_ps = sem("v_ps")
        v_out = sem("v_out")
        mx_ready = sem("mx_ready")
        mx_free = sem("mx_free")
        nm_ready = sem("nm_ready")
        mb_ready = sem("mb_ready")
        m_ready = sem("m_ready")
        s_ready = sem("s_ready")
        e_ready = sem("e_ready")
        pv_free = sem("pv_free")
        adda_free = sem("adda_free")
        addb_free = sem("addb_free")
        vst_ready = [sem("vst_ready0"), sem("vst_ready1")]
        zero_a = sem("zero_a")
        zero_b = sem("zero_b")
        sum_ready = sem("sum_ready")
        rs_ready = sem("rs_ready")
        rs_used = sem("rs_used")
        odd_ready = sem("odd_ready")
        acc_free = sem("acc_free")
        xst_ready = [sem("xst_ready0"), sem("xst_ready1")]
        o_ready = sem("o_ready")
        o_stored = [sem("o_stored0"), sem("o_stored1")]

        MAT_LOADS = [(w, i, h, h) for w, i in ((gate_w, WG), (proj_w, WP), (v_w, WV)) for h in (0, 1)]
        MAT_LOADS += [(w, WQK + h, r, h) for r, w in enumerate((q_w, k_w)) for h in (0, 1)]

        def taps(t):
            dy, dx = divmod(t, 7)
            return dy, dx

        def window(t, r0, rows):
            dy, dx = taps(t)
            return hp[:, r0 + dy:r0 + dy + rows, dx:dx + W]

        def blk(b, j):
            return NBLK * b + j

        def group_of(i):
            return 2 * i[0] + i[1] // GP

        def pair0(b, j):
            return NPAIR * blk(b, j)

        def keys_moved(eng, b):
            for n in range(NPIECE):
                eng.wait_ge(k_moved[n], 32 * (b + 1))
            eng.wait_ge(k2_moved, 16 * NPIECE * (b + 1))

        block = ctx.enter_context(nc.Block())

        @block.sync
        def _(sp):
            def load_x(b):
                for band, (lo, hi) in enumerate(((0, PAD + BAND), (PAD + BAND, XR))):
                    for h in (0, 1):
                        a, z = max(lo, PAD * (1 - h)), min(hi, XR - PAD * h)
                        r = a - PAD + HR * h
                        sp.dma_start(xs[C * h:C * h + C, a:z, :], x[b, :, r:r + z - a, :]).then_inc(x_ready[band], 16)

            for par in (0, 1):
                sp.sem_inc(o_stored[par], 32)
            load_x(0)
            sp.dma_start(prm[:], per_channel[:, :]).then_inc(prm_in, 16)
            sp.wait_ge(const_ready, 2)
            for w, i, rh, ch in MAT_LOADS:
                sp.dma_start(wnat[C * rh:C * rh + C, i, C * ch:C * ch + C], w[:, :]).then_inc(mat_in, 16)

            def spread_qk(b):
                for n in range(NPIECE):
                    cols = slice(n * PIECE * CH, (n + 1) * PIECE * CH)
                    if n == 0:
                        sp.wait_ge(hi_ready, 2 * NCH * b + 1)
                        for h in (0, 1):
                            sp.dma_start(Q0[C * h:C * h + C, :], Q1[0:C, 0:CH]).then_inc(q_first, 16)
                    sp.wait_ge(lo_ready, 2 * NCH * b + (n + 1) * PIECE)
                    sp.dma_start(K1[0:C, cols], Q1[C:P, cols]).then_inc(k_moved[n], 16)
                    sp.dma_start(K1[C:P, cols], Q2[C:P, cols]).then_inc(k_moved[n], 16)
                    sp.dma_start(K2[0:C, cols], Q1[C:P, cols]).then_inc(k2_moved, 16)
                keys_moved(sp, b)
                sp.dma_start(Q1[C:P, :], Q1[0:C, :]).then_inc(q_moved, 16)

            def load_v(b, j, par, d, gg):
                g = 2 * gg + d
                n = blk(b, j) * NG + g
                slot = (par + d) % 2
                if not (isinstance(n, int) and n < 2):
                    sp.wait_ge(pv_free, GP * n)
                sp.dma_start(flat(vst[:, slot, :, :]), x1[:, bass.ds(g * (2 * GP * C), 2 * GP * C)]
                             ).then_inc(vst_ready[slot], 16)

            def attend(b, j, par, store):
                if b == 0 and isinstance(j, int) and j == 0:
                    for g in range(NG - 1):
                        load_v(b, j, par, g % 2, g // 2)
                else:
                    with sp.Fori(0, NG // 2) as gg:
                        for d in (0, 1):
                            load_v(b, j, par, d, gg)
                load_v(b, j, par, 0, NG // 2)
                if not (b == 0 and isinstance(j, int) and j < 2):
                    sp.wait_ge(o_ready, blk(b, j))
                for h in (0, 1):
                    sp.dma_start(xst[C * h:C * h + C, par, :], x1_dram[b, :, bass.ds(j * CH + h * HCH, HCH)]
                                 ).then_inc(xst_ready[par], 16)
                if store:
                    store_out(b, j - 2, par)

            def store_out(b, j, par):
                sp.wait_ge(o_ready, blk(b, j) + 2)
                for h in (0, 1):
                    sp.dma_start(out[b, :, bass.ds(j * CH + h * HCH, HCH)], ot[C * h:C * h + C, par, :]
                                 ).then_inc(o_stored[par], 16)

            for b in range(B):
                sp.wait_ge(x1_ready, NCH * (b + 1))
                if b + 1 < B:
                    load_x(b + 1)
                for h in (0, 1):
                    sp.dma_start(x1_dram[b, :, h * NHALF:(h + 1) * NHALF], x1[C * h:C * h + C, :]).then_inc(x1_stored, 16)
                spread_qk(b)
                sp.wait_ge(x1_stored, 32 * (b + 1))
                sp.wait_ge(v_out, NCH * (b + 1))
                attend(b, 0, 0, False)
                attend(b, 1, 1, False)
                with sp.Fori(1, NBLK // 2) as jj:
                    for par in (0, 1):
                        attend(b, 2 * jj + par, par, True)
                store_out(b, NBLK - 2, 0)
                store_out(b, NBLK - 1, 1)
            for par in (0, 1):
                sp.wait_ge(o_stored[par], 32 * (B * NBLK // 2 + 1))

        @block.gpsimd
        def _(pool):
            nc.gpsimd.memset(ident[:], 0.0).then_inc(pool_step, 1)
            nc.gpsimd.memset(ones[:], 1.0).then_inc(const_ready, 1)
            nc.gpsimd.memset(flat(wnat), 0.0).then_inc(const_ready, 1)
            pool.wait_ge(pool_step, 1)
            nc.gpsimd.affine_select(out=ident[:], in_=ident[:], compare_op=ALU.not_equal, fill=1.0, base=0,
                                    pattern=[[-1, P]], channel_multiplier=1).then_inc(const_ready, 1)
            nc.gpsimd.memset(flat(hp[:]), 0.0).then_inc(hp_zero, 1)
            nc.gpsimd.memset(zero16[:], 0.0).then_inc(const_ready, 1)
            pool.wait_ge(const_ready, 5)
            nc.gpsimd.memset(K2[C:P, :], ONE).then_inc(const_ready, 1)
            nc.gpsimd.sem_inc(adda_free, POOL_ADDS)
            for k in range(1, POOL_TAPS):
                for h in (0, 1):
                    pool.wait_ge(prod_ready, 2 * k + h + 1)
                    if k > 1:
                        pool.wait_ge(prod_added, 2 * (k - 2) + h + 1)
                    at = x1[:, h * (NHALF // 2):(h + 1) * (NHALF // 2)]
                    nc.gpsimd.tensor_tensor(at, at, prod[:, h, :], ALU.add).then_inc(prod_added, 1)
            pool.wait_ge(wstat_ready, 1)
            nc.gpsimd.partition_all_reduce(wmax[:], wstat[:], P, RMAX).then_inc(wmax_ready, 1)

            def add_a(b, j, par, i):
                n = pair0(b, j) + 2 * GP * i[0] + i[1]
                done = POOL_ADDS * (blk(b, j) * NG + group_of(i) + 1) + POOL_DONE[i[1] % GP]
                pool.wait_ge(e_ready, n + 2)
                for t in (0, 1) if i[1] % GP in POOL_ODD else (0,):
                    pool.wait_ge(adda_free, done + t)
                    nc.gpsimd.tensor_tensor(accA[:, par, :], accA[:, par, :], E[:, i[1] % NSLOT, t, :], ALU.add
                                            ).then_inc(adda_free, 1)

            def total(b, j, par):
                pool.wait_ge(addb_free, DVE_ADDS * (NG * (blk(b, j) + 1) + 1))
                pool.wait_ge(adda_free, POOL_ADDS * (NG * (blk(b, j) + 1) + 1))
                pool.wait_ge(rs_ready, blk(b, j) + 1)
                nc.gpsimd.tensor_tensor(accS[:], accA[:, par, :], accB[:, par, :], ALU.add).then_inc(sum_ready, 1)

            def attend(b, j, par, first=False, last=False):
                with pool.Fori(0, NG // 2) as gg:
                    for p in range(2 * GP):
                        add_a(b, j, par, (gg, p))
                for p in range(GP):
                    if p == 0 and not first:
                        total(b, j - 1, 1 - par)
                    if p == 1 and not first:
                        pool.wait_ge(sum_ready, blk(b, j))
                    add_a(b, j, par, (NG // 2, p))
                    if p == 1 and not last:
                        nc.gpsimd.memset(accA[:, 1 - par, :], 0.0).then_inc(zero_a, 1)
                    if p == 2 and not last:
                        pool.wait_ge(zero_a, blk(b, j) + 2)

            for b in range(B):
                for c in range(NCH):
                    pool.wait_ge(sig_ready, NCH * b + c + 1)
                    at = f[:, c * CH:(c + 1) * CH]
                    nc.gpsimd.tensor_tensor(at, at, gs[:, c % 3, :], ALU.mult).then_inc(fg_ready, 1)
                pool.wait_ge(hmax_ready, b + 1)
                nc.gpsimd.partition_all_reduce(bnd[:, 1:2], bnd[:, 0:1], P, RMAX).then_inc(hmax_all, 1)
                for c in range(2 * NCH):
                    n = 2 * NCH * b + c
                    cols = slice(c * CH, (c + 1) * CH)
                    pool.wait_ge(t_ready, n + 1)
                    pool.wait_ge(hi_ready, n + 1)
                    nc.gpsimd.tensor_tensor(Q2[:, cols], T[:, c % 4, :], Q1[:, cols], ALU.subtract).then_inc(lo_ready, 1)
                if b:
                    pool.wait_ge(sum_ready, blk(b, 0))
                nc.gpsimd.memset(accA[:, 0, :], 0.0).then_inc(zero_a, 1)
                pool.wait_ge(zero_a, blk(b, 0) + 1)
                attend(b, 0, 0, first=True)
                with pool.Fori(0, (NBLK - 2) // 2) as jj:
                    attend(b, 2 * jj + 1, 1)
                    attend(b, 2 * jj + 2, 0)
                attend(b, NBLK - 1, 1, last=True)
                total(b, NBLK - 1, 1)

        @block.scalar
        def _(act):
            act.sem_inc(e_ready, 1)
            def exponentials(b, j, i):
                n = pair0(b, j) + 2 * GP * i[0] + i[1]
                slot, buf, r = i[1] % NSLOT, i[1] % 2, i[1] % GP
                group = NG * blk(b, j) + group_of(i)
                act.wait_ge(s_ready, n + 1)
                act.wait_ge(pv_free, n + 1)
                act.wait_ge(adda_free, POOL_ADDS * group + POOL_DONE[r + 1])
                act.wait_ge(addb_free, DVE_ADDS * group + DVE_DONE[r + 1])
                nc.scalar.activation(flat(E[:, slot, :, :]), flat(ps[:, S_BANK + 2 * buf:S_BANK + 2 * buf + 2, :]),
                                     ACT.Exp, scale=bnd[:, 6:7]).then_inc(e_ready, 1)

            def move_odd(b, j, par):
                act.wait_ge(pv_free, NSLOT + pair0(b, j) + NPAIR)
                act.wait_ge(o_ready, blk(b, j) + 1)
                for h in (0, 1):
                    nc.scalar.activation(pvt[C * h:C * h + C, :], ps[C:P, ACC_BANK + par, h * HCH:(h + 1) * HCH],
                                         ACT.Copy).then_inc(odd_ready, 1)

            def attend(b, j, par, first=False):
                with act.Fori(0, NG // 2) as gg:
                    for p in range(2 * GP):
                        exponentials(b, j, (gg, p))
                for p in range(GP):
                    exponentials(b, j, (NG // 2, p))
                    if p == 0 and not first:
                        move_odd(b, j - 1, 1 - par)

            def diagonals():
                for t in range(PE_TAPS):
                    a = nc.scalar.activation(diag[:, t, :], ident[:], ACT.Copy,
                                             scale=wc[:, TAPS - PE_TAPS + t:TAPS - PE_TAPS + t + 1])
                a.then_inc(diag_ready, 1)

            act.wait_ge(const_ready, 3)
            act.wait_ge(wc_ready, 1)
            diagonals()
            def root(n):
                act.wait_ge(var_ready, n + 1)
                nc.scalar.activation(var[:, 1:2], var[:, 0:1], ACT.Sqrt).then_inc(root_ready, 1)

            def pad_half(b, h):
                act.wait_ge(aff_ready, 2 * b + 1)
                rows, ch = ((PAD, XR), (0, HR + PAD))[h], slice(C * h, C * h + C)
                nc.scalar.activation(hp[ch, rows[0]:rows[1], PAD:PAD + W], xs[ch, rows[0]:rows[1], :], ACT.Identity,
                                     bias=aff[ch, 1:2], scale=aff[ch, 0:1]).then_inc(hp_act, 1)

            root(0)
            act.wait_ge(hp_zero, 1)
            pad_half(0, 0)
            act.wait_ge(hp_act, 1)
            act.wait_ge(hp_dve, 1)
            for k in range(POOL_TAPS):
                for h in (0, 1):
                    if k >= 2:
                        act.wait_ge(prod_added, 2 * (k - 2) + h + 1)
                    to = x1[:, h * (NHALF // 2):(h + 1) * (NHALF // 2)] if k == 0 else prod[:, h, :]
                    t = DVE_TAPS + k
                    nc.scalar.activation(to.rearrange("p (y x) -> p y x", x=W), window(t, h * (HR // 2), HR // 2),
                                         ACT.Copy, scale=wc[:, t:t + 1]).then_inc(prod_ready, 1)
            for b in range(B):
                if b:
                    act.wait_ge(adda_free, POOL_ADDS * (NG * blk(b, 0) + 1))
                    act.wait_ge(addb_free, DVE_ADDS * (NG * blk(b, 0) + 1))
                for c in range(NCH):
                    n = NCH * b + c
                    act.wait_ge(gate_ready, n + 1)
                    if c >= 3:
                        act.wait_ge(fg_ready, n - 2)
                    nc.scalar.activation(gs[:, c % 3, :], ps[:, c % 3, :], ACT.Sigmoid,
                                         bias=prm[:, GB:GB + 1]).then_inc(sig_ready, 1)
                root(2 * b + 1)
                act.wait_ge(aff_ready, 2 * b + 2)
                nc.scalar.activation(f[:, 0:H_ACT * CH], x1[:, 0:H_ACT * CH], ACT.Identity, bias=aff[:, 3:4],
                                     scale=aff[:, 2:3]).then_inc(h_act, 1)
                act.wait_ge(scale_ready, b + 1)
                for c in range(2 * NCH):
                    n = 2 * NCH * b + c
                    act.wait_ge(qk_ps, n + 1)
                    if n >= 4:
                        act.wait_ge(lo_ready, n - 3)
                    nc.scalar.activation(T[:, c % 4, :], ps[:, c % 3, :], ACT.Identity,
                                         bias=bnd[:, 5:6], scale=bnd[:, 4:5]).then_inc(t_ready, 1)
                    nc.scalar.activation(Q1[:, c * CH:(c + 1) * CH], ps[:, c % 3, :], ACT.Identity,
                                         bias=bnd[:, 5:6], scale=bnd[:, 4:5]).then_inc(hi_ready, 1)
                if b + 1 < B:
                    root(2 * (b + 1))
                act.wait_ge(x1_stored, 32 * (b + 1))
                for g in range(NCH):
                    act.wait_ge(v_ps, NCH * b + g + 1)
                    for h in (0, 1):
                        a = nc.scalar.activation(V[:, h, NQT * g:NQT * g + NQT, :], ps[:, ACC_BANK + g % 2, :].rearrange(
                            "p (t h c) -> p h t c", t=NQT, h=2)[:, h], ACT.Copy)
                    a.then_inc(v_out, 1)
                    if b + 1 < B and g in (2, 5):
                        pad_half(b + 1, g // 3)
                if b + 1 < B:
                    act.wait_ge(v_ps, NCH * (b + 1))
                    nc.scalar.activation(f[:], bsum[:].to_broadcast([P, NHALF]), ACT.Copy).then_inc(conv_step, 1)
                attend(b, 0, 0, first=True)
                with act.Fori(0, (NBLK - 2) // 2) as jj:
                    attend(b, 2 * jj + 1, 1)
                    attend(b, 2 * jj + 2, 0)
                attend(b, NBLK - 1, 1)
                move_odd(b, NBLK - 1, 1)

        @block.vector
        def _(dve):
            steps = [0]

            def chain(ins):
                steps[0] += 1
                ins.then_inc(dve_step, 1)
                dve.wait_ge(dve_step, steps[0])

            dve.sem_inc(acc_free, 4)
            dve.sem_inc(rs_used, 1)
            dve.sem_inc(o_ready, 1)
            dve.sem_inc(mx_free, 2)
            dve.sem_inc(addb_free, DVE_ADDS)
            dve.wait_ge(const_ready, 3)
            nc.vector.tensor_copy(ident16[:], ident[:]).then_inc(const_ready, 1)
            def joint_kernel():
                dve.wait_ge(prm_in, 16)
                for k, src in ((5, w5s), (3, w3s)):
                    o = (7 - k) // 2
                    mid = wc.rearrange("p (y x) -> p y x", x=7)[:, o:o + k, o:o + k]
                    chain(nc.vector.tensor_tensor(mid, mid, src.rearrange("p (y x) -> p y x", x=k), ALU.add))
                chain(nc.vector.tensor_tensor(bsum[:], prm[:, B3:B3 + 1], prm[:, B5:B5 + 1], ALU.add))
                nc.vector.tensor_tensor(bsum[:], bsum[:], prm[:, B7:B7 + 1], ALU.add).then_inc(wc_ready, 1)

            def weight_norms():
                dve.wait_ge(wt_ps, 1)
                nc.vector.tensor_copy(flat(wT[:, 0:4, :]), ps[:, 4, :])
                nc.vector.tensor_copy(wT[:, 4, :], ps[:, 5, 0:P]).then_inc(wt_ready, 1)
                chain(nc.vector.memset(wstat[:], 0.0))
                for k in (0, 1):
                    rows = slice(C * k, C * k + C)
                    nc.vector.tensor_reduce(wstat[rows, k:k + 1], wnat[rows, WQK, :], AX.X, ALU.add,
                                            apply_absolute_value=True)
                    last = nc.vector.tensor_reduce(wstat[rows, 2 + k:3 + k], prm[rows, QKB:QKB + 1], AX.X, ALU.max,
                                                   apply_absolute_value=True)
                last.then_inc(wstat_ready, 1)

            def norm(b, second, gamma, beta, col):
                dve.wait_ge(bn_done, NCH * (2 * b + second + 1))
                nc.vector.bn_aggr(mv[:], bn[:].rearrange("p a b -> p (a b)")).then_inc(st_in, 1)
                dve.wait_ge(st_ps, 4 * b + 2 * second + 1)
                chain(nc.vector.tensor_scalar(tot[:], ps[:, STAT_BANK, 0:2], 1.0 / P, None, ALU.mult))
                chain(nc.vector.tensor_tensor(dev[:, 0:1], mv[:, 0:1], tot[:, 0:1], ALU.subtract))
                nc.vector.tensor_tensor(dev[:, 1:2], dev[:, 0:1], dev[:, 0:1], ALU.mult).then_inc(st_in, 1)
                dve.wait_ge(st_ps, 4 * b + 2 * second + 2)
                chain(nc.vector.scalar_tensor_tensor(out=tot[:, 1:2], in0=ps[:, STAT_BANK, 2:3], scalar=1.0 / P,
                                                     in1=tot[:, 1:2], op0=ALU.mult, op1=ALU.add))
                nc.vector.tensor_scalar(var[:, 0:1], tot[:, 1:2], EPS, None, ALU.add).then_inc(var_ready, 1)
                dve.wait_ge(root_ready, 2 * b + second + 1)
                chain(nc.vector.reciprocal(tot[:, 1:2], var[:, 1:2]))
                chain(nc.vector.tensor_tensor(var[:, 2:3], tot[:, 1:2], tot[:, 1:2], ALU.mult))
                chain(nc.vector.tensor_tensor(var[:, 2:3], var[:, 2:3], var[:, 0:1], ALU.mult))
                chain(nc.vector.tensor_scalar(var[:, 2:3], var[:, 2:3], -0.5, 1.5, ALU.mult, ALU.add))
                chain(nc.vector.tensor_tensor(tot[:, 1:2], tot[:, 1:2], var[:, 2:3], ALU.mult))
                chain(nc.vector.tensor_tensor(aff[:, col:col + 1], prm[:, gamma:gamma + 1], tot[:, 1:2], ALU.mult))
                chain(nc.vector.tensor_tensor(tot[:, 0:1], tot[:, 0:1], aff[:, col:col + 1], ALU.mult))
                nc.vector.tensor_tensor(aff[:, col + 1:col + 2], prm[:, beta:beta + 1], tot[:, 0:1],
                                        ALU.subtract).then_inc(aff_ready, 1)

            def reduce_max(m, at, c):
                dve.wait_ge(mx_ready, m + 1)
                nc.vector.reduce_max(at, ps[:, MX_BANK + c % 2, :], AX.X).then_inc(mx_free, 1)

            def maxima(b, j):
                f0 = blk(b, j)
                dve.wait_ge(mx_free, 2 + NMX * (f0 + 1))
                nc.vector.reduce_max(m4[:], mxp[:], AX.X).then_inc(m4_done, 1)
                dve.wait_ge(m4_done, f0 + 1)
                dve.wait_ge(mb_ready, f0)
                nc.vector.tensor_scalar(negm[:], m4[:].unsqueeze(2).to_broadcast([P, NQT, P]), -M_ROW, None,
                                        ALU.mult).then_inc(nm_ready, 1)

            def place_maxima(b, j):
                dve.wait_ge(mb_ready, blk(b, j) + 1)
                nc.vector.tensor_copy(Q2[C:P, bass.ds(j * CH, CH)], ps[C:P, MX_BANK, :]).then_inc(m_ready, 1)

            def add_b(b, j, par, i):
                n = pair0(b, j) + 2 * GP * i[0] + i[1]
                dve.wait_ge(e_ready, n + 2)
                dve.wait_ge(addb_free, DVE_ADDS * (NG * blk(b, j) + group_of(i) + 1) + DVE_DONE[i[1] % GP])
                nc.vector.tensor_tensor(accB[:, par, :], accB[:, par, :], E[:, i[1] % NSLOT, 1, :], ALU.add
                                        ).then_inc(addb_free, 1)

            def conv_tap(dy, dx, strip, done):
                dve.wait_ge(conv_step, 1 + done)
                at = f[:, bass.ds(strip * (SROWS * W), SROWS * W)].rearrange("p (y x) -> p y x", x=W)
                src = flat(hp[:])[:, bass.ds((strip * SROWS + dy) * HW_, SROWS * HW_)]
                nc.vector.scalar_tensor_tensor(out=at, in0=src.rearrange("p (y x) -> p y x", x=HW_)[:, :, dx:dx + W],
                                               scalar=wc[:, bass.ds(7 * dy + dx, 1)], in1=at,
                                               op0=ALU.mult, op1=ALU.add).then_inc(conv_step, 1)

            def attend(b, j, par, first=False, last=False, jhalf=None, taps=(), done=0):
                m0 = NMX * (blk(b, j) + 1)
                with dve.Fori(0, NG // 2) as gg:
                    c = 0
                    for p in range(2 * GP):
                        for _ in range(0 if last else 2):
                            reduce_max(m0 + NBLK * gg + c, mxp_at(gg, c), c)
                            c += 1
                        if p % GP not in POOL_ODD:
                            add_b(b, j, par, (gg, p))
                        if p % GP == GP - 1 and not last:
                            reduce_max(m0 + NBLK * gg + c, mxp_at(gg, c), c)
                            c += 1
                        for k, (dy, dx, strip) in enumerate(taps):
                            if TAP_AT[len(taps)][k] == p:
                                conv_tap(dy, dx, strip + gg, done + len(taps) * gg + k)
                if not last:
                    maxima(b, j + 1)
                for p in range(GP):
                    if p == 1 and not last:
                        place_maxima(b, j + 1)
                    if p == 2 and not last:
                        dve.wait_ge(zero_b, blk(b, j) + 2)
                    if p not in POOL_ODD:
                        add_b(b, j, par, (NG // 2, p))
                    if p == 1 and not first:
                        finish(b, j - 1, 1 - par, jhalf)
                    if p == 1 and not last:
                        dve.wait_ge(sum_ready, blk(b, j))
                        nc.vector.memset(accB[:, 1 - par, :], 0.0).then_inc(zero_b, 1)

            def attend_and_convolve(b):
                half = STRIPS // 2
                both = lambda dys, dx: [(dy, dx, s) for dy in dys for s in (0, half)]
                loop = [[(0, dx, s) for dx in range(5)] for s in (0, half)]
                head = both((0, 1), 5)
                tail = [both((2, 3), 5) + [(4, 5, 0)], both((5, 6), 5) + [(4, 5, half)], both(range(7), 6)]
                done = 0
                dve.wait_ge(hp_act, 2 * b + 3)
                attend(b, 0, 0, first=True, taps=head, done=done)
                done += half * len(head)
                each = half * len(loop[0])
                with dve.Fori(0, 7) as jj:
                    for par in (1, 0):
                        taps = [(jj, dx, s) for _, dx, s in loop[1 - par]]
                        attend(b, 2 * jj + 2 - par, par, jhalf=jj, taps=taps,
                               done=done + each * (2 * jj + 1 - par))
                done += 7 * 2 * each
                for j, taps in zip(range(NBLK - 3, NBLK), tail):
                    attend(b, j, j % 2, last=(j == NBLK - 1), taps=taps, done=done)
                    done += half * len(taps)
                assert done == TAPS * STRIPS

            def mxp_at(gg, c):
                return flat(mxp[:])[:, bass.ds(NBLK * gg + c, 1)]

            def finish(b, j, par, jhalf):
                f0 = blk(b, j)
                done = (b * (NBLK // 2) + (j // 2 if jhalf is None else jhalf)) * 32
                dve.wait_ge(odd_ready, 2 * f0 + 2)
                for h in (0, 1):
                    rows = slice(C * h, C * h + C)
                    nc.vector.tensor_tensor(pvt[rows, :], ps[0:C, ACC_BANK + par, h * HCH:(h + 1) * HCH], pvt[rows, :],
                                            ALU.add).then_inc(acc_free, 1)
                dve.wait_ge(rs_ready, f0 + 2)
                nc.vector.reciprocal(rec[:], ps[:, MX_BANK + 1, 0:HCH]).then_inc(rs_used, 1)
                dve.wait_ge(acc_free, 2 * f0 + 6)
                dve.wait_ge(rs_used, f0 + 2)
                nc.vector.tensor_tensor(pvt[:], pvt[:], rec[:], ALU.mult).then_inc(norm_done, 1)
                dve.wait_ge(norm_done, f0 + 1)
                dve.wait_ge(xst_ready[par], done + 32)
                dve.wait_ge(o_stored[par], done + 32)
                nc.vector.scalar_tensor_tensor(out=ot[:, par, :], in0=pvt[:], scalar=prm[:, VB:VB + 1],
                                               in1=xst[:, par, :], op0=ALU.add, op1=ALU.add).then_inc(o_ready, 1)

            def x_stats(b, c):
                if c == 0:
                    dve.wait_ge(x_ready[0], 32 * (b + 1))
                if (c + 1) * CH > BAND * W >= c * CH:
                    dve.wait_ge(x_ready[1], 32 * (b + 1))
                nc.vector.bn_stats(bn[:, c, :], x_in[:, c * CH:(c + 1) * CH]).then_inc(bn_done, 1)

            def pad():
                norm(0, 0, G1, B1, 0)
                dve.wait_ge(aff_ready, 1)
                dve.wait_ge(hp_zero, 1)
                nc.vector.tensor_scalar(hp[C:P, 0:HR + PAD, PAD:PAD + W], xs[C:P, 0:HR + PAD, :], aff[C:P, 0:1],
                                        aff[C:P, 1:2], ALU.mult, ALU.add).then_inc(hp_dve, 1)
                dve.wait_ge(hp_act, 1)
                dve.wait_ge(hp_dve, 1)

            def add_chunk(c):
                dve.wait_ge(cps_ready, c + 1)
                at = f[:, c * CROWS * W:(c + 1) * CROWS * W]
                nc.vector.tensor_tensor(at, at, ps[:, c % 4, 0:CROWS * W], ALU.add).then_inc(cps_out, 1)
                dve.wait_ge(cps_out, c + 1)

            for c in range(NCH):
                x_stats(0, c)
                if c == 0:
                    joint_kernel()
            pad()
            for b in range(B):
                if b == 0:
                    f3 = f[:].rearrange("p (y x) -> p y x", x=W)
                    chain(nc.vector.tensor_scalar(f3, window(0, 0, HR), wc[:, 0:1], bsum[:], ALU.mult, ALU.add))
                    added = 0
                    for t in range(1, DVE_TAPS):
                        chain(nc.vector.scalar_tensor_tensor(out=f3, in0=window(t, 0, HR), scalar=wc[:, t:t + 1],
                                                             in1=f3, op0=ALU.mult, op1=ALU.add))
                        if t >= FIRST_ADD and t % 2 and added < CCH:
                            add_chunk(added)
                            added += 1
                    while added < CCH:
                        add_chunk(added)
                        added += 1
                    weight_norms()
                    dve.wait_ge(prod_added, 2 * (POOL_TAPS - 1))
                    dve.wait_ge(cps_out, CCH)
                    for c in range(NCH):
                        at = slice(c * CH, (c + 1) * CH)
                        nc.vector.tensor_tensor(f[:, at], f[:, at], x1[:, at], ALU.add).then_inc(f_ready, 1)
                else:
                    dve.wait_ge(conv_step, 1 + TAPS * STRIPS)

                def x1_stats(c):
                    dve.wait_ge(x1_ready, NCH * b + c + 1)
                    at = x1[:, c * CH:(c + 1) * CH]
                    nc.vector.bn_stats(bn[:, c, :], at).then_inc(bn_done, 1)
                    nc.vector.tensor_reduce(x1_max[:, c:c + 1], at, AX.X, ALU.max,
                                            apply_absolute_value=True).then_inc(x1_maxed, 1)

                for c in range(NCH):
                    n = NCH * b + c
                    dve.wait_ge(proj_ready, n + 1)
                    at = x1[:, c * CH:(c + 1) * CH]
                    nc.vector.scalar_tensor_tensor(out=at, in0=ps[:, PROJ_BANK + c % 2, :], scalar=prm[:, PB:PB + 1],
                                                   in1=x_in[:, c * CH:(c + 1) * CH], op0=ALU.add,
                                                   op1=ALU.add).then_inc(x1_ready, 1)
                    if c:
                        x1_stats(c - 1)
                x1_stats(NCH - 1)
                norm(b, 1, G2, B2, 2)
                dve.wait_ge(x1_maxed, NCH * (b + 1))
                dve.wait_ge(aff_ready, 2 * b + 2)
                chain(nc.vector.tensor_reduce(bnd[:, 0:1], x1_max[:], AX.X, ALU.max))
                chain(nc.vector.tensor_reduce(aff_abs[:], aff[:, 2:4].unsqueeze(2), AX.X, ALU.max,
                                              apply_absolute_value=True))
                nc.vector.scalar_tensor_tensor(out=bnd[:, 0:1], in0=bnd[:, 0:1], scalar=aff_abs[:, 0:1],
                                               in1=aff_abs[:, 1:2], op0=ALU.mult, op1=ALU.add).then_inc(hmax_ready, 1)
                nc.vector.tensor_scalar(f[:, H_ACT * CH:], x1[:, H_ACT * CH:], aff[:, 2:3], aff[:, 3:4], ALU.mult,
                                        ALU.add).then_inc(h_dve, 1)
                dve.wait_ge(hmax_all, b + 1)
                dve.wait_ge(wmax_ready, 1)
                chain(nc.vector.scalar_tensor_tensor(out=bnd[:, 2:4], in0=wmax[:, 0:2], scalar=bnd[:, 1:2],
                                                     in1=wmax[:, 2:4], op0=ALU.mult, op1=ALU.add))
                chain(nc.vector.tensor_scalar(bnd[:, 2:4], bnd[:, 2:4], 1e-12, 1.0 / QK_TOP, ALU.max, ALU.mult))
                for k in (0, 1):
                    rows = slice(C * k, C * k + C)
                    chain(nc.vector.reciprocal(bnd[rows, 4:5], bnd[rows, 2 + k:3 + k]))
                chain(nc.vector.tensor_tensor(bnd[:, 5:6], bnd[:, 4:5], prm[:, QKB:QKB + 1], ALU.mult))
                chain(nc.vector.tensor_tensor(bnd[:, 6:7], bnd[:, 2:3], bnd[:, 3:4], ALU.mult))
                nc.vector.tensor_scalar(bnd[:, 6:7], bnd[:, 6:7], C ** -0.5, None, ALU.mult).then_inc(scale_ready, 1)
                if b + 1 < B:
                    for c in range(NCH):
                        x_stats(b + 1, c)
                for c in range(NMX):
                    kc, qt = divmod(c, NQT)
                    if b + 1 < B and c == MX_BESIDE:
                        norm(b + 1, 0, G1, B1, 0)
                    reduce_max(NMX * blk(b, 0) + c, mxp[:, qt, kc:kc + 1], c)
                maxima(b, 0)
                keys_moved(dve, b)
                place_maxima(b, 0)
                if b:
                    dve.wait_ge(sum_ready, blk(b, 0))
                nc.vector.memset(accB[:, 0, :], 0.0).then_inc(zero_b, 1)
                dve.wait_ge(zero_b, blk(b, 0) + 1)
                if b + 1 == B:
                    attend(b, 0, 0, first=True)
                    with dve.Fori(0, (NBLK - 2) // 2) as jj:
                        attend(b, 2 * jj + 1, 1, jhalf=jj)
                        attend(b, 2 * jj + 2, 0, jhalf=jj)
                    attend(b, NBLK - 1, 1, last=True)
                else:
                    attend_and_convolve(b)
                finish(b, NBLK - 1, 1, None)

        @block.tensor
        def _(pe):
            pe.sem_inc(rs_ready, 1)
            pe.sem_inc(pv_free, NSLOT)
            pe.wait_ge(const_ready, 6)

            def transpose_weights():
                pe.wait_ge(mat_in, 16 * len(MAT_LOADS))
                for i in range(5):
                    a = nc.tensor.transpose(ps[:, 4 + i // 4, (i % 4) * P:(i % 4 + 1) * P], wnat[:, i, :], ident[:])
                a.then_inc(wt_ps, 1)

            def stats(n):
                pe.wait_ge(st_in, n + 1)
                nc.tensor.matmul(ps[:, STAT_BANK, 0:2], ones[:], mv[:], start=True, stop=True).then_inc(st_ps, 1)
                pe.wait_ge(st_in, n + 2)
                nc.tensor.matmul(ps[:, STAT_BANK, 2:3], ones[:], dev[:, 1:2], start=True, stop=True).then_inc(st_ps, 1)

            def scores(b, j, i, n, peers):
                base, p = i
                buf = p % 2
                if peers is not None:
                    pe.wait_ge(e_ready, peers + 1)
                for t in (0, 1):
                    k = bass.ds((2 * GP * base + p) * 2 * P + t * P, P)
                    dst = ps[:, S_BANK + 2 * buf + t, :]
                    nc.tensor.matmul(dst, K1[:, k], Q1[:, bass.ds(j * CH, CH)], start=True, stop=False)
                    a = nc.tensor.matmul(dst, K2[:, k], Q2[:, bass.ds(j * CH, CH)], start=False, stop=True)
                a.then_inc(s_ready, 1)

            def weigh(b, par, p, n, slot):
                pe.wait_ge(e_ready, n + 2)
                for t in (0, 1):
                    a = nc.tensor.matmul(ps[C * t:C * t + C, ACC_BANK + par, :], vst[:, slot, 2 * (p % GP) + t, :],
                                         E[:, p % NSLOT, t, :], start=False, stop=False, skip_group_check=True)
                a.then_inc(pv_free, 1)

            def max_scores(queries, kc, m, c):
                pe.wait_ge(mx_free, m + 1)
                nc.tensor.matmul(ps[:, MX_BANK + c % 2, :], queries, K1[:, kc * CH:(kc + 1) * CH],
                                 start=True, stop=True).then_inc(mx_ready, 1)

            def spread_maxima(b, j):
                pe.wait_ge(nm_ready, blk(b, j) + 1)
                for q in range(NQT):
                    a = nc.tensor.matmul(ps[:, MX_BANK, q * P:(q + 1) * P], negm[:, q, :], ident16[:], start=True, stop=True)
                a.then_inc(mb_ready, 1)

            def row_sums(b, j):
                pe.wait_ge(sum_ready, blk(b, j) + 1)
                for h in (0, 1):
                    a = nc.tensor.matmul(ps[C * h:C * h + C, MX_BANK + 1, 0:HCH], ones[:, 0:C],
                                         accS[:, h * HCH:(h + 1) * HCH], start=True, stop=True)
                a.then_inc(rs_ready, 1)

            def vst_wait(b, j, par, jhalf, d, gg):
                slot = (par + d) % 2
                n = NG * (blk(b, 0) // 2) + NG * jhalf + (NG * par + d) // 2 + gg
                pe.wait_ge(vst_ready[slot], 16 * (n + 1))
                return slot

            def attend(b, j, par, jhalf, first=False, last=False):
                n0 = pair0(b, j)
                m0 = NMX * (blk(b, j) + 1)
                pe.wait_ge(acc_free, 2 * blk(b, j) + 2)
                if not first:
                    pe.wait_ge(rs_used, blk(b, j))
                nc.tensor.matmul(ps[:, ACC_BANK + par, :], zero16[:], Q1[:, 0:CH], start=True, stop=True)
                with pe.Fori(0, NG // 4) as half:
                    for gg in (2 * half, 2 * half + 1):
                        c = 0
                        queries = None if last else Q1[:, bass.ds((j + 1) * CH + gg * P, P)]
                        for p in range(2 * GP):
                            n = n0 + 2 * GP * gg + p
                            scores(b, j, (gg, p + 1), n + 1, n)
                            for _ in range(0 if last else 2):
                                max_scores(queries, c, m0 + NBLK * gg + c, c)
                                c += 1
                            if p % GP == 0:
                                slot = vst_wait(b, j, par, jhalf, p // GP, gg)
                            weigh(b, par, p, n, slot)
                            if p % GP == GP - 1 and not last:
                                max_scores(queries, c, m0 + NBLK * gg + c, c)
                                c += 1
                slot = vst_wait(b, j, par, jhalf, NG - 1, 0)
                for p in range(GP):
                    n = n0 + NPAIR - GP + p
                    if p < GP - 1:
                        scores(b, j, (NG // 2, p + 1), n + 1, n)
                    elif not last:
                        pe.wait_ge(m_ready, blk(b, j) + 2)
                        scores(b, j + 1, (0, 0), n + 1, n)
                    if p == 1 and not last:
                        spread_maxima(b, j + 1)
                    if p == 2 and not first:
                        row_sums(b, j - 1)
                    weigh(b, par, p, n, slot)

            stats(0)
            pe.wait_ge(diag_ready, 1)
            pe.wait_ge(hp_act, 1)
            pe.wait_ge(hp_dve, 1)
            for c in range(CCH):
                if c >= 4:
                    pe.wait_ge(cps_out, c - 3)
                for t in range(PE_TAPS):
                    a = nc.tensor.matmul(ps[:, c % 4, 0:CROWS * W].rearrange("p (y x) -> p y x", x=W),
                                         diag[:, t, :], window(TAPS - PE_TAPS + t, c * CROWS, CROWS),
                                         start=(t == 0), stop=(t == PE_TAPS - 1))
                a.then_inc(cps_ready, 1)
            transpose_weights()
            pe.wait_ge(wt_ready, 1)

            for b in range(B):
                if b:
                    pe.wait_ge(e_ready, pair0(b, 0) + 1)
                def gate(c):
                    n = NCH * b + c
                    if b == 0:
                        pe.wait_ge(f_ready, c + 1)
                    if c >= 3:
                        pe.wait_ge(sig_ready, n - 2)
                    nc.tensor.matmul(ps[:, c % 3, :], wT[:, WG, :], f[:, c * CH:(c + 1) * CH], start=True,
                                     stop=True).then_inc(gate_ready, 1)

                if b:
                    pe.wait_ge(conv_step, 1 + TAPS * STRIPS)
                gate(0)
                gate(1)
                if b:
                    row_sums(b - 1, NBLK - 1)
                for c in range(NCH):
                    n = NCH * b + c
                    if c + 2 < NCH:
                        gate(c + 2)
                    pe.wait_ge(fg_ready, n + 1)
                    if c >= 2:
                        pe.wait_ge(x1_ready, n - 1)
                    nc.tensor.matmul(ps[:, PROJ_BANK + c % 2, :], wT[:, WP, :], f[:, c * CH:(c + 1) * CH], start=True,
                                     stop=True).then_inc(proj_ready, 1)
                stats(4 * b + 2)
                pe.wait_ge(h_act, b + 1)

                def block0_maxima(c):
                    kc, qt = divmod(c, NQT)
                    if c == 0:
                        pe.wait_ge(o_ready, NBLK * b + 1)
                        pe.wait_ge(q_first, 32 * (b + 1))
                    if c % (NQT * PIECE) == 0:
                        pe.wait_ge(k_moved[kc // PIECE], 32 * (b + 1))
                    max_scores(Q0[:, qt * P:(qt + 1) * P], kc, NMX * blk(b, 0) + c, c)

                done = 0
                for c in range(2 * NCH):
                    h, cc = divmod(c, NCH)
                    n = 2 * NCH * b + c
                    if c == H_ACT:
                        pe.wait_ge(h_dve, b + 1)
                    if c >= 3:
                        pe.wait_ge(hi_ready, n - 2)
                    nc.tensor.matmul(ps[:, c % 3, :], wT[:, WQK + h, :], f[:, cc * CH:(cc + 1) * CH], start=True,
                                     stop=True).then_inc(qk_ps, 1)
                    if c >= MX_FROM:
                        for _ in range(2):
                            block0_maxima(done)
                            done += 1
                assert done == MX_BESIDE
                if b + 1 < B:
                    stats(4 * (b + 1))
                each = -(-(NMX - done) // NCH)
                for g in range(NCH):
                    if g >= 2:
                        pe.wait_ge(v_out, NCH * b + g - 1)
                    for q in range(max(each, NQT)):
                        if q < each and done < NMX:
                            block0_maxima(done)
                            done += 1
                        if q < NQT:
                            t = NQT * g + q
                            a = nc.tensor.matmul(ps[:, ACC_BANK + g % 2, q * P:(q + 1) * P],
                                                 f[:, t * P:(t + 1) * P], wT[:, WV, :], start=True, stop=True)
                            if q == NQT - 1:
                                a.then_inc(v_ps, 1)
                spread_maxima(b, 0)
                keys_moved(pe, b)
                pe.wait_ge(q_moved, 16 * (b + 1))
                if b + 1 < B:
                    pe.wait_ge(aff_ready, 2 * b + 3)
                pe.wait_ge(v_out, NCH * (b + 1))
                pe.wait_ge(m_ready, blk(b, 0) + 1)
                scores(b, 0, (0, 0), pair0(b, 0), None)
                attend(b, 0, 0, 0, first=True)
                with pe.Fori(0, (NBLK - 2) // 2) as jj:
                    attend(b, 2 * jj + 1, 1, jj)
                    attend(b, 2 * jj + 2, 0, jj + 1)
                attend(b, NBLK - 1, 1, NBLK // 2 - 1, last=True)
            row_sums(B - 1, NBLK - 1)


def kernel(**inputs):
    import concourse.bacc as bacc
    from concourse.bass_utils import run_bass_kernel_spmd

    nc = bacc.Bacc("TRN2", target_bir_lowering=False, num_devices=1)
    raw = {n.removeprefix("L0_conv_"): np.asarray(a) for n, a in inputs.items()}
    both = ("n1_g", "n1_b", "n2_g", "n2_b", "b3", "b5", "b7", "gate_b", "proj_b", "v_b")
    columns = [np.tile(raw[n], 2)[:, None] for n in both]
    columns += [np.concatenate([raw["q_b"], raw["k_b"]])[:, None]]
    columns += [np.tile(raw[n].reshape(C, -1), (2, 1)) for n in ("w3", "w5", "w7")]
    given = {"x": raw["x"], "per_channel": np.concatenate(columns, axis=1)}
    given.update({n: raw[n] for n in ("gate_w", "proj_w", "q_w", "k_w", "v_w")})
    arrays, args = {}, []
    for name, a in given.items():
        arrays[f"in_{name}"] = a = np.ascontiguousarray(a)
        args.append(nc.dram_tensor(f"in_{name}", a.shape, mybir.dt.from_np(a.dtype), kind="ExternalInput").ap())
    out = nc.dram_tensor("out", (B, C, N), F32, kind="ExternalOutput").ap()
    program(nc, *args, out)
    r = run_bass_kernel_spmd(nc, [arrays], core_ids=[0])
    return r.results[0]["out"].reshape(B, C, H, W)
```
